# Optimizing a Trainium2 kernel written in Bass

```python
import numpy as np
import jax
import jax.numpy as jnp

def _softmax(x, axis=-1):
    return jax.nn.softmax(x, axis=axis)

def _gelu(x):
    return jax.nn.gelu(x, approximate=True)

def _silu(x):
    return jax.nn.silu(x)

def _sigmoid(x):
    return jax.nn.sigmoid(x)

def _layernorm(x, axis=-1, eps=1e-05):
    m = jnp.mean(x, axis=axis, keepdims=True)
    v = jnp.var(x, axis=axis, keepdims=True)
    return (x - m) / jnp.sqrt(v + eps)

def _scatter_add(tgt, idx, src, axis=0):
    return tgt.at[idx].add(src)

def _segment_sum(src, seg, n):
    return jax.ops.segment_sum(src, seg, n)
kernel_name = 'mk_adaln_d1_jaxref_r4_d2d41f'

def setup_inputs(seed: int=0):
    np.random.seed(seed)
    _w = jnp.asarray

    def _L0_attn_setup():
        import jax, jax.numpy as jnp
        import numpy as np
        B, S, D = (4, 1024, 512)
        IDENTITY_WEIGHT = 0.5
        ROT_DIM = D // 2

        def _layernorm(x, gamma, beta, eps=1e-05):
            mu = jnp.mean(x, axis=-1, keepdims=True)
            var = jnp.var(x, axis=-1, keepdims=True)
            return (x - mu) * jax.lax.rsqrt(var + eps) * gamma + beta

        def _rotary(t, rot_dim, theta=10000.0):
            seq = t.shape[-2]
            inv_freq = 1.0 / theta ** (jnp.arange(0, rot_dim, 2, dtype=jnp.float32) / rot_dim)
            freqs = jnp.arange(seq, dtype=jnp.float32)[:, None] * inv_freq[None, :]
            freqs = jnp.repeat(freqs, 2, axis=-1)
            cos, sin = (jnp.cos(freqs), jnp.sin(freqs))
            t_rot, t_pass = (t[..., :rot_dim], t[..., rot_dim:])
            x1, x2 = (t_rot[..., 0::2], t_rot[..., 1::2])
            rot_half = jnp.stack([-x2, x1], axis=-1).reshape(t_rot.shape)
            return jnp.concatenate([t_rot * cos + rot_half * sin, t_pass], axis=-1)

        def _cos_sim(x):
            return x / jnp.linalg.norm(x, axis=-1, keepdims=True)
        key = jax.random.key(seed)
        ks = jax.random.split(key, 3)
        scale = 0.02
        return {'X': jax.random.normal(ks[0], (B, S, D), jnp.float32), 'W_in': jax.random.normal(ks[1], (D, 3 * D), jnp.float32) * scale, 'b_in': jnp.zeros((3 * D,), jnp.float32), 'W_out': jax.random.normal(ks[2], (D, D), jnp.float32) * scale, 'b_out': jnp.zeros((D,), jnp.float32), 'gamma': jnp.ones((D,), jnp.float32), 'beta': jnp.zeros((D,), jnp.float32)}
    _L0_attn_in = _L0_attn_setup()

    def _L0_ffn_setup():
        import jax, jax.numpy as jnp
        import numpy as np
        DIM = 512
        N_EXPERTS = 8
        TOP_K = 2
        key = jax.random.key(seed)
        ks = jax.random.split(key, 5)
        x = jax.random.normal(ks[0], (4, 1024, DIM), dtype=jnp.float32)
        W_up = jax.random.normal(ks[1], (DIM, DIM), dtype=jnp.float32) * (1.0 / np.sqrt(DIM))
        W_down = jax.random.normal(ks[2], (DIM, DIM), dtype=jnp.float32) * (1.0 / np.sqrt(DIM))
        W_gate = jax.random.normal(ks[3], (N_EXPERTS, DIM), dtype=jnp.float32) * (1.0 / np.sqrt(DIM))
        W_expert = jax.random.normal(ks[4], (DIM, DIM), dtype=jnp.float32) * (1.0 / np.sqrt(DIM))
        return {'x': x, 'W_up': W_up, 'W_down': W_down, 'W_gate': W_gate, 'W_expert': W_expert}
    _L0_ffn_in = _L0_ffn_setup()
    _L0_c = _w((lambda *s: np.random.randn(*s).astype(np.float32) * 0.05)(4, 512))
    _L0_wmod = _w((lambda *s: np.random.randn(*s).astype(np.float32) * 0.05)(512, 6 * 512) * 512 ** (-0.5))
    _d = {'L0_attn_X': _L0_attn_in['X'], 'L0_attn_W_in': _L0_attn_in['W_in'], 'L0_attn_b_in': _L0_attn_in['b_in'], 'L0_attn_W_out': _L0_attn_in['W_out'], 'L0_attn_b_out': _L0_attn_in['b_out'], 'L0_attn_gamma': _L0_attn_in['gamma'], 'L0_attn_beta': _L0_attn_in['beta'], 'L0_ffn_W_up': _L0_ffn_in['W_up'], 'L0_ffn_W_down': _L0_ffn_in['W_down'], 'L0_ffn_W_gate': _L0_ffn_in['W_gate'], 'L0_ffn_W_expert': _L0_ffn_in['W_expert'], 'L0_c': _L0_c, 'L0_wmod': _L0_wmod}
    _x0 = _d['L0_attn_X']
    _d['L0_attn_X'] = jax.random.normal(jax.random.fold_in(jax.random.key(seed), 1), (4, 512, 512), dtype=_x0.dtype)
    del _x0
    return _d

def reference(L0_attn_X, L0_attn_W_in, L0_attn_b_in, L0_attn_W_out, L0_attn_b_out, L0_attn_gamma, L0_attn_beta, L0_ffn_W_up, L0_ffn_W_down, L0_ffn_W_gate, L0_ffn_W_expert, L0_c, L0_wmod):

    def _L0_attn_ref(X, W_in, b_in, W_out, b_out, gamma, beta):
        import jax, jax.numpy as jnp
        import numpy as np
        B, S, D = (4, 1024, 512)
        IDENTITY_WEIGHT = 0.5
        ROT_DIM = D // 2

        def _layernorm(x, gamma, beta, eps=1e-05):
            mu = jnp.mean(x, axis=-1, keepdims=True)
            var = jnp.var(x, axis=-1, keepdims=True)
            return (x - mu) * jax.lax.rsqrt(var + eps) * gamma + beta

        def _rotary(t, rot_dim, theta=10000.0):
            seq = t.shape[-2]
            inv_freq = 1.0 / theta ** (jnp.arange(0, rot_dim, 2, dtype=jnp.float32) / rot_dim)
            freqs = jnp.arange(seq, dtype=jnp.float32)[:, None] * inv_freq[None, :]
            freqs = jnp.repeat(freqs, 2, axis=-1)
            cos, sin = (jnp.cos(freqs), jnp.sin(freqs))
            t_rot, t_pass = (t[..., :rot_dim], t[..., rot_dim:])
            x1, x2 = (t_rot[..., 0::2], t_rot[..., 1::2])
            rot_half = jnp.stack([-x2, x1], axis=-1).reshape(t_rot.shape)
            return jnp.concatenate([t_rot * cos + rot_half * sin, t_pass], axis=-1)

        def _cos_sim(x):
            return x / jnp.linalg.norm(x, axis=-1, keepdims=True)
        Xn = _layernorm(X, gamma, beta)
        QKV = Xn @ W_in + b_in
        Q, K, V = jnp.split(QKV, 3, axis=-1)
        K = _rotary(K, ROT_DIM)
        V = _rotary(V, ROT_DIM)
        A = jnp.sum(_cos_sim(K) * _cos_sim(V), axis=-2)
        A = (1.0 - IDENTITY_WEIGHT) * A + IDENTITY_WEIGHT
        Y = A[:, None, :] * Q
        Y = Y @ W_out + b_out
        return Y + X

    def _L0_ffn_ref(x, W_up, W_down, W_gate, W_expert):
        import jax, jax.numpy as jnp
        import numpy as np
        DIM = 512
        N_EXPERTS = 8
        TOP_K = 2
        logits = jnp.einsum('bsd,ed->bse', x, W_gate)
        routing_weights, selected_experts = jax.lax.top_k(logits, TOP_K)
        shared_out = jnp.einsum('bsd,od->bso', jax.nn.relu(jnp.einsum('bsd,od->bso', x, W_up)), W_down)
        rw = jax.nn.softmax(routing_weights, axis=-1)
        expert_out = jnp.einsum('bsd,do->bso', x, W_expert)
        moe_out = jnp.sum(rw, axis=-1, keepdims=True) * expert_out
        return shared_out + moe_out
    x = L0_attn_X
    mod = (_silu(L0_c) @ L0_wmod).reshape(L0_c.shape[0], 6, 1, -1)
    sa, ca, ga, sb, cb, gb = (mod[:, 0], mod[:, 1], mod[:, 2], mod[:, 3], mod[:, 4], mod[:, 5])
    ga = (2 * (ga >= 0) - 1) * jnp.maximum(jnp.abs(ga), 0.25)
    gb = (2 * (gb >= 0) - 1) * jnp.maximum(jnp.abs(gb), 0.25)
    h = _layernorm(x, axis=-1) * (1 + ca) + sa
    x = x + ga * _L0_attn_ref(h, L0_attn_W_in, L0_attn_b_in, L0_attn_W_out, L0_attn_b_out, L0_attn_gamma, L0_attn_beta)
    h = _layernorm(x, axis=-1) * (1 + cb) + sb
    x = x + gb * _L0_ffn_ref(h, L0_ffn_W_up, L0_ffn_W_down, L0_ffn_W_gate, L0_ffn_W_expert)
    return x

_drawn_inputs = setup_inputs


def setup_inputs(seed=0):
    import zlib

    import numpy as np

    out = dict(_drawn_inputs(seed))
    spreads = {'L0_attn_b_in': (0.0, 0.8),
     'L0_attn_b_out': (0.0, 0.352),
     'L0_attn_gamma': (1.0, 0.6),
     'L0_attn_beta': (0.0, 2.0)}
    factors = {'L0_ffn_W_gate': 64.0}
    for name, (base, spread) in spreads.items():
        noise = np.random.default_rng([zlib.crc32(name.encode()), seed]).standard_normal(out[name].shape)
        drawn = base * np.exp(spread * noise) if base else spread * noise
        out[name] = jnp.asarray(drawn.astype(out[name].dtype))
    for name, factor in factors.items():
        out[name] = (out[name] * factor).astype(out[name].dtype)
    return out
```

```python
import concourse.bass as bass
from concourse import mybir
from contextlib import ExitStack

P = 128
B, S, D = 4, 512, 512
NT = S // P
NC = D // P
ROT = D // 4
NE = 8
NCOMP = 6
EPS = 1e-5
MIN_GATE = 0.25
IDENTITY_WEIGHT = 0.5

COL_GAMMA, COL_BETA, COL_BQ, COL_C, COL_WG = 0, NC, 2 * NC, 3 * NC, 3 * NC + NC * B
COLS = COL_WG + NC * NE

WK, WV, WQ, WO = range(4)
WUP, WEXP, WDOWN = WK, WV, WQ

KV_BANKS = ((0, 1), (2, 3))
Q_BANKS = (4, 5, 0, 1)
O_BANKS = (2, 3, 4, 5)
U_BANKS = (4, 5)
E_BANKS = (0, 1, 2, 3)
D_BANKS = (4, 5)
T_BANKS = (6, 7)
SMALL_BANK = 7


def build(nc, X, cols, ident, rot, w, wmod, brow, out):
    f32 = mybir.dt.float32
    f32r = mybir.dt.float32r
    ALU = mybir.AluOpType
    ACT = mybir.ActivationFunctionType

    x_rows = X.rearrange("b (t p) d -> (b t) p d", p=P)
    out_rows = out.rearrange("b (t p) d -> (b t) p d", p=P)
    x_batch = X.rearrange("b (t p) d -> b p t d", p=P)
    out_batch = out.rearrange("b (t p) d -> b p t d", p=P)
    ROW_CA, ROW_SA, ROW_GA, ROW_GB = range(4)
    mod_rows = nc.dram_tensor("mod_rows", (4, B, D), f32, kind="Internal").ap()

    ctx = ExitStack()
    with ctx:
        def sb(name, shape, dt=f32):
            return ctx.enter_context(nc.sbuf_tensor(name, shape, dt))

        def sem(name):
            return ctx.enter_context(nc.semaphore(name))

        w_hi = sb("w_hi", [P, 4, NC, D], f32r)
        w_lo = sb("w_lo", [P, 4, NC, D], f32r)
        wg_r = sb("wg_r", [P, NC, 2 * NE], f32r)
        stage = sb("stage", [P, 2, NC * D])
        t_hi = sb("t_hi", [P, NC, S], f32r)
        t_lo = sb("t_lo", [P, NC, S], f32r)
        g_hi = sb("g_hi", [P, NC, S], f32r)
        g_lo = sb("g_lo", [P, NC, S], f32r)
        xs = sb("xs", [P, B * NT * D])
        h1 = sb("h1", [P, NT * D])
        z = sb("z", [P, NT, D])
        ca_bc = sb("ca_bc", [P, D])
        sa_bc = sb("sa_bc", [P, D])
        gate_bc = sb("gate_bc", [P, B * D])
        bkv_bc = sb("bkv_bc", [P, 2, D])
        bo_bc = sb("bo_bc", [P, D])
        rot_sb = sb("rot_sb", [P, NT, 2 * ROT])
        kv = sb("kv", [P, 2, 2, D])
        prod = sb("prod", [P, D + 2 * ROT])
        cross = sb("cross", [P, 2 * ROT])
        acc = sb("acc", [P, D + 2 * ROT])
        full = sb("full", [P, 2, S])
        tmp = sb("tmp", [P, 2, D])
        es = kv[:, :, 0, :]
        rows = kv[0:B, :, 1, :]
        col = sb("col", [P, COLS])
        idn = sb("idn", [P, P])
        half = sb("half", [P, 4])
        expo = sb("expo", [P, NT])
        sc = sb("sc", [P, NC * B])
        sc_t = sb("sc_t", [P, 3, NC * B])
        cb_col = sb("cb_col", [P, B * NC])
        sb_col = sb("sb_col", [P, B * NC])
        xst = sb("xst", [P, NT, 6])
        xmv = sb("xmv", [P, NT, 2])
        xve = sb("xve", [P, NT])
        xrs = sb("xrs", [P, NT])
        hst = sb("hst", [P, NT, 6])
        hmv = sb("hmv", [P, NT, 2])
        hve = sb("hve", [P, NT])
        hrs = sb("hrs", [P, NT])
        hnm = sb("hnm", [P, NT])
        nsq = sb("nsq", [P, 2, 2])
        rnm = sb("rnm", [P, 2, 2])
        wgt = sb("wgt", [P, 2])
        sqj = sb("sqj", [P, D], mybir.dt.bfloat16)
        a_col = sb("a_col", [P, NC])
        ab_col = sb("ab_col", [P, NC])
        lg2 = sb("lg2", [P, NT, 2 * NE])
        lg = sb("lg", [P, NT, NE])
        top8 = sb("top8", [P, NT, 8])
        tdif = sb("tdif", [P, NT, 2])
        tex = sb("tex", [P, NT, 2])
        tsum = sb("tsum", [P, NT])
        trec = sb("trec", [P, NT])
        trw = sb("trw", [P, NT, 2])
        rsum = sb("rsum", [P, NT])
        ps = ctx.enter_context(nc.psum_tensor("ps", [P, 8, 512], f32))

        col_in = sem("col_in")
        const_in = sem("const_in")
        x_in = sem("x_in")
        wm_in = [sem(f"wm_in{i}") for i in range(NCOMP)]
        w_in = [sem(f"w_in{i}") for i in range(7)]
        row_out = sem("row_out")
        ca_in = sem("ca_in")
        ga_in = sem("ga_in")
        gb_in = sem("gb_in")
        waits_done = sem("waits_done")
        cst = sem("cst")
        c_exp = sem("c_exp")
        c_steps = sem("c_steps")
        wg_hi_s = sem("wg_hi_s")
        mod_ps = sem("mod_ps")
        mod_sb = sem("mod_sb")
        whi = sem("whi")
        wlo = sem("wlo")
        xst_s, xmv_s, xve_s, xrs_s = (sem(n) for n in ("xst_s", "xmv_s", "xve_s", "xrs_s"))
        u_s = sem("u_s")
        h1_s = sem("h1_s")
        hst_s, hmv_s, hve_s, hrs_s, hnm_s = (sem(n) for n in ("hst_s", "hmv_s", "hve_s", "hrs_s", "hnm_s"))
        z_s = sem("z_s")
        t_ps, t_full, t_his, t_los = (sem(n) for n in ("t_ps", "t_full", "t_his", "t_los"))
        r_s = sem("r_s")
        kv_ps, kv_sb = sem("kv_ps"), sem("kv_sb")
        nsq_s, rnm_s, wgt_s = sem("nsq_s"), sem("rnm_s"), sem("wgt_s")
        kprod, kcross, krot, kacc = (sem(n) for n in ("kprod", "kcross", "krot", "kacc"))
        a_ps, a_sb, ab_sb = sem("a_ps"), sem("a_sb"), sem("ab_sb")
        q_ps, q_full, q_his, q_los = (sem(n) for n in ("q_ps", "q_full", "q_his", "q_los"))
        o_ps, o_y, x2_s = sem("o_ps"), sem("o_y"), sem("x2_s")
        lg_ps, lg_s, top_s, ex_s, rsum_s = (sem(n) for n in ("lg_ps", "lg_s", "top_s", "ex_s", "rsum_s"))
        lg_sum = sem("lg_sum")
        u_ps, u_his, u_los = (sem(n) for n in ("u_ps", "u_his", "u_los"))
        e_ps, es_s = sem("e_ps"), sem("es_s")
        d_ps, d_y, out_s = sem("d_ps"), sem("d_y"), sem("out_s")
        out_dma = sem("out_dma")

        block = ctx.enter_context(nc.Block())

        FREE_NSQ, FREE_RNM, FREE_ACC, FREE_O, FREE_DY = 4, 2, 1, NT, 4

        def wait(eng, s, v):
            if not (isinstance(v, int) and v <= 0):
                eng.wait_ge(s, v)

        def tok(b, t):
            return bass.ds((b * NT + t) * D, D)

        def wait_apart(eng, s, v):
            eng.wait_ge(s, v)
            eng.sem_inc(waits_done, 1)

        N_CONST = 4 * 16
        W_ORDER = (WK, WV, WQ, WO, WUP, WEXP, WDOWN)

        W_SLOT = (0, 1, 0, 1, 0, 1, 1)

        @block.sync
        def _(sp):
            sp.dma_start(col[:], cols).then_inc(col_in, 16)
            sp.dma_start(xs[:, 2 * NT * D:3 * NT * D], wmod[1]).then_inc(wm_in[1], 16)
            sp.dma_start(xs[:, 3 * NT * D:4 * NT * D], wmod[0]).then_inc(wm_in[0], 16)
            sp.dma_start(xs[:, 0:NT * D].rearrange("p (t d) -> p t d", t=NT), x_batch[0]).then_inc(x_in, 16)
            sp.dma_start(idn[:], ident).then_inc(const_in, 16)
            sp.dma_start(stage[:, 0, :], w[0]).then_inc(w_in[0], 16)
            sp.dma_start(stage[:, 1, :], w[1]).then_inc(w_in[1], 16)
            sp.dma_start(xs[:, NT * D:2 * NT * D], wmod[2]).then_inc(wm_in[2], 16)
            sp.dma_start(rot_sb[:], rot).then_inc(const_in, 16)
            sp.dma_start(bkv_bc[:].rearrange("p a d -> p (a d)"), brow[0:1, 0:2 * D].to_broadcast([P, 2 * D])).then_inc(const_in, 16)
            sp.dma_start(bo_bc[:], brow[0:1, 2 * D:3 * D].to_broadcast([P, D])).then_inc(const_in, 16)
            sp.wait_ge(mod_sb, 2)
            sp.dma_start(mod_rows[ROW_CA], rows[:, 0, :]).then_inc(row_out, 16)
            sp.dma_start(mod_rows[ROW_SA], rows[:, 1, :]).then_inc(row_out, 16)
            sp.wait_ge(row_out, 32)
            sp.dma_start(ca_bc[:], mod_rows[ROW_CA, 0:1, :].to_broadcast([P, D])).then_inc(ca_in, 16)
            sp.dma_start(sa_bc[:], mod_rows[ROW_SA, 0:1, :].to_broadcast([P, D])).then_inc(ca_in, 16)
            sp.wait_ge(mod_sb, 7)
            sp.dma_start(mod_rows[ROW_GA], rows[:, 1, :]).then_inc(row_out, 16)
            sp.wait_ge(row_out, 48)
            for b in range(B):
                sp.dma_start(gate_bc[:, b * D:(b + 1) * D],
                             mod_rows[ROW_GA, b:b + 1, :].to_broadcast([P, D])).then_inc(ga_in, 16)
            sp.wait_ge(wlo, 1)
            sp.wait_ge(whi, 1)
            sp.dma_start(stage[:, 0, :], w[2]).then_inc(w_in[2], 16)
            sp.wait_ge(wlo, 2)
            sp.dma_start(stage[:, 1, :], w[3]).then_inc(w_in[3], 16)

            with sp.Fori(0, B - 1) as b:
                sp.wait_ge(x_in, b * 16 + 16)
                sp.wait_ge(mod_ps, 3)
                sp.dma_start(xs[:, bass.ds((b + 1) * NT * D, NT * D)].rearrange("p (t d) -> p t d", t=NT),
                             x_batch[bass.ds(b + 1, 1)].rearrange("o p t d -> (o p) t d")).then_inc(x_in, 16)
                sp.wait_ge(h1_s, b * NT + NT)
                sp.dma_start(ca_bc[:], mod_rows[ROW_CA, bass.ds(b + 1, 1), :].to_broadcast([P, D])).then_inc(ca_in, 16)
                sp.dma_start(sa_bc[:], mod_rows[ROW_SA, bass.ds(b + 1, 1), :].to_broadcast([P, D])).then_inc(ca_in, 16)
            sp.wait_ge(wlo, 3)
            sp.dma_start(stage[:, 0, :], wmod[4]).then_inc(wm_in[4], 16)
            sp.wait_ge(wlo, 4)
            sp.dma_start(stage[:, 1, :], wmod[3]).then_inc(wm_in[3], 16)
            sp.wait_ge(mod_ps, 4)
            sp.dma_start(stage[:, 0, :], w[4]).then_inc(w_in[4], 16)
            sp.wait_ge(mod_ps, 5)
            sp.dma_start(stage[:, 1, :], w[5]).then_inc(w_in[5], 16)
            sp.wait_ge(wlo, 5)
            sp.dma_start(stage[:, 0, :], wmod[5]).then_inc(wm_in[5], 16)
            sp.wait_ge(wlo, 6)
            sp.dma_start(stage[:, 1, :], w[6]).then_inc(w_in[6], 16)
            sp.wait_ge(mod_sb, 14)
            sp.dma_start(mod_rows[ROW_GB], rows[:, 1, :]).then_inc(row_out, 16)
            sp.wait_ge(row_out, 64)
            sp.wait_ge(x2_s, B * NT)
            for b in range(B):
                sp.dma_start(gate_bc[:, b * D:(b + 1) * D],
                             mod_rows[ROW_GB, b:b + 1, :].to_broadcast([P, D])).then_inc(gb_in, 16)
            with sp.Fori(0, B * NT) as i:
                sp.wait_ge(out_s, i + 1)
                sp.dma_start(out_rows[bass.ds(i, 1)].rearrange("o p d -> (o p) d"),
                             xs[:, bass.ds(i * D, D)]).then_inc(out_dma, 16)
            sp.wait_ge(out_dma, B * NT * 16)

        @block.gpsimd
        def _(pool):
            def power(dst, src, n, s):
                nc.gpsimd.tensor_tensor(dst, src, expo[:, 0:n], ALU.pow).then_inc(s, 1)

            def rstd_x(g):
                pool.wait_ge(xve_s, g + 1)
                power(xrs[:], xve[:], NT, xrs_s)

            def rstd_h(g):
                pool.wait_ge(hve_s, g + 1)
                wait(pool, z_s, g * NT)
                power(hrs[:], hve[:], NT, hrs_s)

            def weight(b, t):
                pool.wait_ge(nsq_s, (b * NT + t) * 2 + 2 + FREE_NSQ)
                power(rnm[:, t % 2, :], nsq[:, t % 2, :], 2, rnm_s)
                pool.wait_ge(rnm_s, b * NT + t + 1 + FREE_RNM)
                nc.gpsimd.tensor_tensor(wgt[:, t % 2:t % 2 + 1], rnm[:, t % 2, 0:1], rnm[:, t % 2, 1:2],
                                        ALU.mult).then_inc(wgt_s, 1)

            def residual(g, t):
                base = (g * NT + t) * 3
                h = h1[:, t * D:(t + 1) * D]
                pool.wait_ge(z_s, g * NT + t + 1)
                nc.gpsimd.tensor_tensor(h, h, bo_bc[:], ALU.add).then_inc(r_s, 1)
                wait_apart(pool, r_s, base + 1)
                nc.gpsimd.tensor_tensor(h, h, gate_bc[:, bass.ds(g * D, D)], ALU.mult).then_inc(r_s, 1)
                wait_apart(pool, r_s, base + 2)
                nc.gpsimd.tensor_tensor(xs[:, tok(g, t)], xs[:, tok(g, t)], h, ALU.add).then_inc(r_s, 1)

            def attention(b, last):
                weight(b, 0)
                if not last:
                    rstd_x(b + 1)
                weight(b, 1)
                weight(b, 2)
                rstd_h(b + 1)
                weight(b, 3)
                if not last:
                    for t in range(NT):
                        residual(b + 1, t)

            pool.sem_inc(rnm_s, FREE_RNM)
            pool.wait_ge(cst, 4)
            rstd_x(0)
            rstd_h(0)
            pool.wait_ge(ga_in, B * 16)
            pool.wait_ge(const_in, N_CONST)
            for t in range(NT):
                residual(0, t)
            with pool.Fori(0, B - 1) as b:
                attention(b, False)
            attention(B - 1, True)
            with pool.Fori(0, B - 1) as b:
                rstd_h(b + B + 1)

        @block.scalar
        def _(act):
            def split_hi(i):
                act.wait_ge(w_in[i], 16)
                if i == 4:
                    act.wait_ge(kv_ps, B * NT)
                if i == 6:
                    act.wait_ge(q_ps, B * NC)
                slot = W_SLOT[i]
                nc.scalar.activation(w_hi[:, W_ORDER[i]].rearrange("p k n -> p (k n)"), stage[:, slot, :],
                                     ACT.Copy).then_inc(whi, 1)

            def norm_sums(b, t):
                act.wait_ge(kv_sb, b * NT + t + 1)
                act.wait_ge(rnm_s, b * NT + t - 1 + FREE_RNM)
                for i in range(2):
                    act.wait_ge(nsq_s, (b * NT + t) * 2 + i + FREE_NSQ)
                    nc.scalar.activation(sqj[:], kv[:, t % 2, i, :], ACT.Square,
                                         accum_out=nsq[:, t % 2, i:i + 1]).then_inc(nsq_s, 1)

            def normalise(g):
                act.wait_ge(hnm_s, g + 1)
                wait(act, t_ps, g * NC)
                for t in range(NT):
                    src = h1[:, t * D:(t + 1) * D] if first_ln(g) else xs[:, tok(g_off(g), t)]
                    nc.scalar.activation(z[:, t, :], src, ACT.Identity, bias=hnm[:, t:t + 1],
                                         scale=hrs[:, t:t + 1]).then_inc(z_s, 1)

            def t_evac(g, c, ffn, after_q=False):
                n = g * NC + c
                act.wait_ge(t_ps, n + 1)
                if after_q and c < 2:
                    act.wait_ge(q_los, n - 1)
                else:
                    wait(act, t_los, n - 1)
                if ffn:
                    j = bass.ds((g - B) * NC + c, 1)
                    scale, bias = cb_col[:, j], sb_col[:, j]
                else:
                    scale, bias = col[:, COL_GAMMA + c:COL_GAMMA + c + 1], col[:, COL_BETA + c:COL_BETA + c + 1]
                nc.scalar.activation(full[:, c % 2, :], ps[:, T_BANKS[c % 2], :], ACT.Identity,
                                     bias=bias, scale=scale).then_inc(t_full, 1)
                act.wait_ge(t_full, n + 1)
                nc.scalar.activation(t_hi[:, c, :], full[:, c % 2, :], ACT.Copy).then_inc(t_his, 1)

            def q_evac(b, c):
                n = b * NC + c
                act.wait_ge(q_ps, n + 1)
                if c == 0:
                    act.wait_ge(ab_sb, b + 1)
                if c >= 2:
                    act.wait_ge(q_los, n - 1)
                else:
                    act.wait_ge(t_los, n + 3)
                nc.scalar.activation(full[:, c % 2, :], ps[:, Q_BANKS[c], :], ACT.Identity,
                                     bias=ab_col[:, c:c + 1], scale=a_col[:, c:c + 1]).then_inc(q_full, 1)
                act.wait_ge(q_full, n + 1)
                nc.scalar.activation(g_hi[:, c, :], full[:, c % 2, :], ACT.Copy).then_inc(q_his, 1)

            def u_evac(b, c):
                act.wait_ge(u_ps, b * NC + c + 1)
                nc.scalar.activation(g_hi[:, c, :], ps[:, U_BANKS[c % 2], :], ACT.Relu).then_inc(u_his, 1)

            def e_evac(b, t):
                act.wait_ge(e_ps, b * NT + t + 1)
                if t == 0:
                    act.wait_ge(rsum_s, b + 1)
                act.wait_ge(d_y, (b * NT + t - 2) * 2 + 1 + FREE_DY)
                nc.scalar.activation(es[:, t % 2, :], ps[:, E_BANKS[t], :], ACT.Copy,
                                     scale=rsum[:, t:t + 1]).then_inc(es_s, 1)

            def attention(b, last):
                for t in range(NT):
                    norm_sums(b, t)
                state["first"] = not last
                normalise(b + 1)
                for c in range(NC):
                    q_evac(b, c)
                if last:
                    split_hi(4)
                    split_hi(5)
                    act.wait_ge(mod_sb, 9)
                for c in range(NC):
                    if c == 0:
                        act.wait_ge(q_ps, b * NC + NC)
                    t_evac(b + 1, c, last, after_q=True)

            state = {"first": True}

            def first_ln(g):
                return state["first"]

            def g_off(g):
                return g - B

            act.sem_inc(nsq_s, FREE_NSQ)
            act.wait_ge(col_in, 16)
            nc.scalar.activation(sc_t[:, 0, :], col[:, COL_C:COL_C + NC * B], ACT.Exp, scale=-1.0).then_inc(c_exp, 1)
            nc.scalar.activation(wg_r[:, :, 0:NE], col[:, COL_WG:COLS].rearrange("p (k e) -> p k e", k=NC),
                                 ACT.Copy).then_inc(wg_hi_s, 1)
            split_hi(0)
            split_hi(1)
            normalise(0)
            for c in range(NC):
                t_evac(0, c, False)
            split_hi(2)
            split_hi(3)
            with act.Fori(0, B - 1) as b:
                attention(b, False)
            attention(B - 1, True)
            split_hi(6)

            def ffn(b, last):
                act.wait_ge(top_s, b * 5 + 5)
                nc.scalar.activation(tex[:], tdif[:], ACT.Exp).then_inc(ex_s, 1)
                for c in range(NC):
                    u_evac(b, c)
                if not last:
                    normalise(b + B + 1)
                for c in range(NC):
                    if not last:
                        if c == 0:
                            act.wait_ge(e_ps, b * NT + NT)
                        t_evac(b + B + 1, c, True)
                    if c % 2 or last:
                        e_evac(b, c // 2 if not last else c)
                if not last:
                    e_evac(b, 2)
                    e_evac(b, 3)

            state["first"] = False
            with act.Fori(0, B - 1) as b:
                ffn(b, False)
            ffn(B - 1, True)

        @block.vector
        def _(dve):
            v = nc.vector

            def split_lo(i):
                dve.wait_ge(whi, i + 1)
                if i == 4:
                    dve.wait_ge(kv_ps, B * NT)
                slot = W_SLOT[i]
                r = W_ORDER[i]
                v.tensor_tensor(w_lo[:, r].rearrange("p k n -> p (k n)"), stage[:, slot, :],
                                w_hi[:, r].rearrange("p k n -> p (k n)").bitcast(f32), ALU.subtract).then_inc(wlo, 1)

            def x_stats(g):
                dve.wait_ge(x_in, g * 16 + 16)
                for t in range(NT):
                    v.bn_stats(xst[:, t, :], xs[:, tok(g, t)]).then_inc(xst_s, 1)
                for t in range(NT):
                    wait_apart(dve, xst_s, g * NT + t + 1)
                    v.bn_aggr(xmv[:, t, :], xst[:, t, :]).then_inc(xmv_s, 1)
                dve.wait_ge(xmv_s, g * NT + NT)
                v.tensor_scalar(xve[:], xmv[:, :, 1], EPS, None, ALU.add).then_inc(xve_s, 1)

            def h_rows(g, t):
                n = g * NT + t
                if t == 0:
                    dve.wait_ge(ca_in, g * 32 + 32)
                    dve.wait_ge(xrs_s, g + 1)
                    wait(dve, r_s, g * NT * 3)
                v.scalar_tensor_tensor(tmp[:, t % 2, :], xs[:, tok(g, t)], xmv[:, t, 0:1], ca_bc[:],
                                       ALU.subtract, ALU.mult).then_inc(u_s, 1)
                dve.wait_ge(u_s, n + 1)
                v.scalar_tensor_tensor(h1[:, t * D:(t + 1) * D], tmp[:, t % 2, :], xrs[:, t:t + 1], sa_bc[:],
                                       ALU.mult, ALU.add).then_inc(h1_s, 1)
                dve.wait_ge(h1_s, n + 1)
                v.bn_stats(hst[:, t, :], h1[:, t * D:(t + 1) * D]).then_inc(hst_s, 1)

            def x2_rows(g, t):
                v.bn_stats(hst[:, t, :], xs[:, tok(g - B, t)]).then_inc(hst_s, 1)

            def h_aggr(g):
                for t in range(NT):
                    wait_apart(dve, hst_s, g * NT + t + 1)
                    v.bn_aggr(hmv[:, t, :], hst[:, t, :]).then_inc(hmv_s, 1)
                dve.wait_ge(hmv_s, g * NT + NT)
                v.tensor_scalar(hve[:], hmv[:, :, 1], EPS, None, ALU.add).then_inc(hve_s, 1)

            def h_shift(g):
                dve.wait_ge(hrs_s, g + 1)
                v.scalar_tensor_tensor(hnm[:], hmv[:, :, 0], -1.0, hrs[:], ALU.mult, ALU.mult).then_inc(hnm_s, 1)

            def t_split(g, c):
                dve.wait_ge(t_his, g * NC + c + 1)
                v.tensor_tensor(t_lo[:, c, :], full[:, c % 2, :], t_hi[:, c, :].bitcast(f32),
                                ALU.subtract).then_inc(t_los, 1)

            def kv_rows(b, t):
                n = b * NT + t
                pair = KV_BANKS[t % 2]
                k, val = kv[:, t % 2, 0, :], kv[:, t % 2, 1, :]
                dve.wait_ge(kv_ps, n + 1)
                dve.wait_ge(nsq_s, (n - 1) * 2 + FREE_NSQ)
                v.tensor_tensor(kv[:, t % 2], ps[:, pair[0]:pair[0] + 2, :], bkv_bc[:], ALU.add).then_inc(kv_sb, 1)
                dve.wait_ge(kv_sb, n + 1)
                dve.wait_ge(kacc, n + FREE_ACC)
                v.tensor_tensor(prod[:, 0:D], k, val, ALU.mult).then_inc(kprod, 1)
                v.tensor_tensor(cross[:, 0:ROT], k[:, 0:ROT], val[:, ROT:2 * ROT], ALU.mult).then_inc(kcross, 1)
                v.tensor_tensor(cross[:, ROT:2 * ROT], k[:, ROT:2 * ROT], val[:, 0:ROT], ALU.mult).then_inc(kcross, 1)
                dve.wait_ge(kprod, n + 1)
                v.tensor_tensor(prod[:, D:D + ROT], prod[:, 0:ROT], prod[:, ROT:2 * ROT], ALU.subtract).then_inc(krot, 1)
                dve.wait_ge(kcross, n * 2 + 2)
                v.tensor_tensor(prod[:, D + ROT:D + 2 * ROT], cross[:, 0:ROT], cross[:, ROT:2 * ROT],
                                ALU.add).then_inc(krot, 1)
                dve.wait_ge(krot, n * 3 + 2)
                v.tensor_tensor(prod[:, D:D + 2 * ROT], prod[:, D:D + 2 * ROT], rot_sb[:, t, :],
                                ALU.mult).then_inc(krot, 1)

            def kv_sum(b, t):
                n = b * NT + t
                dve.wait_ge(krot, n * 3 + 3)
                dve.wait_ge(wgt_s, n + 1)
                if t == 0:
                    wait(dve, a_ps, b)
                    v.tensor_scalar(acc[:], prod[:], wgt[:, 0:1], None, ALU.mult).then_inc(kacc, 1)
                else:
                    dve.wait_ge(kacc, n + FREE_ACC)
                    v.scalar_tensor_tensor(acc[:], prod[:], wgt[:, t % 2:t % 2 + 1], acc[:],
                                           ALU.mult, ALU.add).then_inc(kacc, 1)

            def a_evac(b):
                dve.wait_ge(a_ps, b + 1)
                v.tensor_scalar(a_col[:], ps[:, SMALL_BANK, 0:NC], 1.0 - IDENTITY_WEIGHT, IDENTITY_WEIGHT,
                                ALU.mult, ALU.add).then_inc(a_sb, 1)
                dve.wait_ge(a_sb, b + 1)
                v.tensor_tensor(ab_col[:], a_col[:], col[:, COL_BQ:COL_BQ + NC], ALU.mult).then_inc(ab_sb, 1)

            def q_split(b, c):
                dve.wait_ge(q_his, b * NC + c + 1)
                v.tensor_tensor(g_lo[:, c, :], full[:, c % 2, :], g_hi[:, c, :].bitcast(f32),
                                ALU.subtract).then_inc(q_los, 1)

            def o_evac(b, t):
                n = b * NT + t
                dve.wait_ge(o_ps, n + 1)
                v.tensor_tensor(tmp[:, t % 2, :], ps[:, O_BANKS[t], :], gate_bc[:, bass.ds(b * D, D)],
                                ALU.mult).then_inc(o_y, 1)
                dve.wait_ge(o_y, n + 1 + FREE_O)
                if t == 0:
                    dve.wait_ge(r_s, b * NT * 3 + NT * 3)
                v.tensor_tensor(xs[:, tok(b, t)], xs[:, tok(b, t)], tmp[:, t % 2, :], ALU.add).then_inc(x2_s, 1)

            def attention(b, last):
                for t in range(NT):
                    kv_rows(b, t)
                    if not last:
                        if t == 0:
                            x_stats(b + 1)
                        elif t == 1:
                            h_rows(b + 1, 0)
                            h_rows(b + 1, 1)
                        elif t == 2:
                            h_rows(b + 1, 2)
                            h_rows(b + 1, 3)
                            h_aggr(b + 1)
                        else:
                            h_shift(b + 1)
                    else:
                        if t == 0:
                            dve.wait_ge(x2_s, NT)
                            for j in range(NT):
                                x2_rows(B, j)
                            h_aggr(B)
                        if t == 2:
                            h_shift(B)
                    kv_sum(b, t)
                a_evac(b)
                for c in range(NC):
                    q_split(b, c)
                if last:
                    split_lo(4)
                    split_lo(5)
                for c in range(NC):
                    t_split(b + 1, c)
                for t in range(NT):
                    o_evac(b, t)

            def gate_rows(bank, done):
                sign, g = rows[:, 0, :], rows[:, 1, :]
                v.tensor_copy(g, ps[0:B, bank, :]).then_inc(mod_sb, 1)
                dve.wait_ge(mod_sb, done + 1)
                v.tensor_scalar(sign, g, 0.0, 2.0, ALU.is_ge, ALU.mult).then_inc(mod_sb, 1)
                dve.wait_ge(mod_sb, done + 2)
                v.scalar_tensor_tensor(g, g, -1.0, g, ALU.mult, ALU.max).then_inc(mod_sb, 1)
                dve.wait_ge(mod_sb, done + 3)
                v.tensor_scalar(g, g, MIN_GATE, None, ALU.max).then_inc(mod_sb, 1)
                dve.wait_ge(mod_sb, done + 4)
                v.scalar_tensor_tensor(g, sign, -1.0, g, ALU.add, ALU.mult).then_inc(mod_sb, 1)

            for s, n in ((kacc, FREE_ACC), (o_y, FREE_O), (d_y, FREE_DY)):
                dve.sem_inc(s, n)
            v.memset(half[:, 0:1], 1.0).then_inc(cst, 1)
            v.memset(half[:, 1:2], 0.5).then_inc(cst, 1)
            v.memset(half[:, 2:3], -0.5).then_inc(cst, 1)
            v.memset(expo[:], -0.5).then_inc(cst, 1)
            dve.wait_ge(c_exp, 1)
            v.tensor_scalar(sc_t[:, 1, :], sc_t[:, 0, :], 1.0, None, ALU.add).then_inc(c_steps, 1)
            dve.wait_ge(c_steps, 1)
            v.reciprocal(sc_t[:, 2, :], sc_t[:, 1, :]).then_inc(c_steps, 1)
            dve.wait_ge(c_steps, 2)
            v.tensor_tensor(sc[:], sc_t[:, 2, :], col[:, COL_C:COL_C + NC * B], ALU.mult).then_inc(c_steps, 1)
            dve.wait_ge(wg_hi_s, 1)
            v.tensor_tensor(wg_r[:, :, NE:2 * NE], col[:, COL_WG:COLS].rearrange("p (k e) -> p k e", k=NC),
                            wg_r[:, :, 0:NE].bitcast(f32), ALU.subtract).then_inc(c_steps, 1)
            x_stats(0)
            dve.wait_ge(mod_ps, 1)
            v.tensor_scalar(rows[:, 0, :], ps[0:B, 0, :], 1.0, None, ALU.add).then_inc(mod_sb, 1)
            dve.wait_ge(mod_ps, 2)
            v.tensor_copy(rows[:, 1, :], ps[0:B, 1, :]).then_inc(mod_sb, 1)
            split_lo(0)
            for t in range(NT):
                h_rows(0, t)
            h_aggr(0)
            h_shift(0)
            split_lo(1)
            dve.wait_ge(mod_ps, 3)
            dve.wait_ge(row_out, 32)
            gate_rows(2, 2)
            for c in range(NC):
                t_split(0, c)
            split_lo(2)
            split_lo(3)
            dve.wait_ge(const_in, N_CONST)
            with dve.Fori(0, B - 1) as b:
                attention(b, False)
            dve.wait_ge(mod_ps, 4)
            v.tensor_scalar(cb_col[:].rearrange("p (b c) -> p c b", c=NC),
                            ps[:, 0, 0:NC * B].rearrange("p (c b) -> p c b", c=NC), 1.0, None, ALU.add).then_inc(mod_sb, 1)
            dve.wait_ge(mod_ps, 5)
            v.tensor_copy(sb_col[:].rearrange("p (b c) -> p c b", c=NC),
                          ps[:, 1, 0:NC * B].rearrange("p (c b) -> p c b", c=NC)).then_inc(mod_sb, 1)
            attention(B - 1, True)
            split_lo(6)
            dve.wait_ge(mod_ps, 6)
            gate_rows(6, 9)

            def routing(b):
                dve.wait_ge(lg_ps, b + 1)
                v.tensor_copy(lg2[:], ps[:, SMALL_BANK, 0:NT * 2 * NE].rearrange("p (t e) -> p t e", t=NT)).then_inc(lg_s, 1)
                dve.wait_ge(lg_s, b * 2 + 1)
                v.tensor_tensor(lg[:], lg2[:, :, 0:NE], lg2[:, :, NE:2 * NE], ALU.add).then_inc(lg_s, 1)
                wait_apart(dve, lg_s, b * 2 + 2)
                for t in range(NT):
                    v.max(top8[:, t, :], lg[:, t, :]).then_inc(top_s, 1)
                dve.wait_ge(top_s, b * 5 + 4)
                v.tensor_tensor(tdif[:], top8[:, :, 0:2], top8[:, :, 0:1].to_broadcast([P, NT, 2]),
                                ALU.subtract).then_inc(top_s, 1)

            def routing_sum(b):
                dve.wait_ge(ex_s, b + 1)
                v.tensor_tensor(tsum[:], tex[:, :, 0], tex[:, :, 1], ALU.add).then_inc(lg_sum, 1)
                dve.wait_ge(lg_sum, b * 3 + 1)
                v.reciprocal(trec[:], tsum[:]).then_inc(lg_sum, 1)
                dve.wait_ge(lg_sum, b * 3 + 2)
                v.tensor_tensor(trw[:], tex[:], trec[:].rearrange("p (t o) -> p t o", o=1).to_broadcast([P, NT, 2]),
                                ALU.mult).then_inc(lg_sum, 1)
                dve.wait_ge(lg_sum, b * 3 + 3)
                v.tensor_tensor(rsum[:], trw[:, :, 0], trw[:, :, 1], ALU.add).then_inc(rsum_s, 1)

            def u_split(b, c):
                dve.wait_ge(u_his, b * NC + c + 1)
                v.scalar_tensor_tensor(g_lo[:, c, :], ps[:, U_BANKS[c % 2], :], 0.0, g_hi[:, c, :].bitcast(f32),
                                       ALU.max, ALU.subtract).then_inc(u_los, 1)

            def d_evac(b, t):
                n = b * NT + t
                y = tmp[:, t % 2, :]
                dve.wait_ge(d_ps, n + 1)
                dve.wait_ge(es_s, n + 1)
                v.tensor_tensor(y, ps[:, D_BANKS[t % 2], :], es[:, t % 2, :], ALU.add).then_inc(d_y, 1)
                dve.wait_ge(d_y, n * 2 + 1 + FREE_DY)
                v.tensor_tensor(y, y, gate_bc[:, bass.ds(b * D, D)], ALU.mult).then_inc(d_y, 1)
                dve.wait_ge(d_y, n * 2 + 2 + FREE_DY)
                v.tensor_tensor(xs[:, tok(b, t)], xs[:, tok(b, t)], y, ALU.add).then_inc(out_s, 1)

            def ffn(b, last):
                routing(b)
                for c in range(NC):
                    u_split(b, c)
                    if not last:
                        x2_rows(b + B + 1, c)
                    if c == 0:
                        routing_sum(b)
                if not last:
                    h_aggr(b + B + 1)
                    h_shift(b + B + 1)
                for c in range(NC):
                    if not last:
                        t_split(b + B + 1, c)
                    if c % 2 or last:
                        d_evac(b, c // 2 if not last else c)
                if not last:
                    d_evac(b, 2)
                    d_evac(b, 3)

            dve.wait_ge(gb_in, B * 16)
            with dve.Fori(0, B - 1) as b:
                ffn(b, False)
            ffn(B - 1, True)

        @block.tensor
        def _(pe):
            mm = nc.tensor.matmul

            def three(dst, l_hi, l_lo, r_hi, r_lo, start, stop):
                mm(dst, l_hi, r_hi, start=start, stop=False)
                mm(dst, l_hi, r_lo, start=False, stop=False)
                return mm(dst, l_lo, r_hi, start=False, stop=stop)

            def weights_ready(i):
                pe.wait_ge(wlo, i + 1)

            def mod_row(bank, src, s):
                pe.wait_ge(s, 16)
                for k in range(NC):
                    last = mm(ps[0:B, bank, :], sc[:, k * B:(k + 1) * B], src[:, k * D:(k + 1) * D],
                              start=(k == 0), stop=(k == NC - 1))
                last.then_inc(mod_ps, 1)

            def mod_col(bank, src, s):
                pe.wait_ge(s, 16)
                for c in range(NC):
                    for k in range(NC):
                        last = mm(ps[:, bank, c * B:(c + 1) * B], src[:, k * D + c * P:k * D + (c + 1) * P],
                                  sc[:, k * B:(k + 1) * B], start=(k == 0), stop=(k == NC - 1))
                last.then_inc(mod_ps, 1)

            def transposes(g, c):
                if c == 0:
                    pe.wait_ge(z_s, g * NT + NT)
                wait(pe, t_full, g * NC + c - 1)
                for t in range(NT):
                    last = nc.tensor.transpose(ps[:, T_BANKS[c % 2], t * P:(t + 1) * P], z[:, t, c * P:(c + 1) * P], idn[:])
                last.then_inc(t_ps, 1)

            def kv_tile(b, t):
                if t == 1:
                    pe.wait_ge(o_y, (b - 1) * NT + 2 + FREE_O)
                if t >= 2:
                    pe.wait_ge(kv_sb, b * NT + t - 1)
                pair = KV_BANKS[t % 2]
                for k in range(NC):
                    if t == 0:
                        pe.wait_ge(t_los, b * NC + k + 1)
                    lo, hi = t_lo[:, k, t * P:(t + 1) * P], t_hi[:, k, t * P:(t + 1) * P]
                    for bank, r in zip(pair, (WK, WV)):
                        last = three(ps[:, bank, :], hi, lo, w_hi[:, r, k, :], w_lo[:, r, k, :], k == 0, k == NC - 1)
                last.then_inc(kv_ps, 1)

            def feature_chunk(bank, r, c, s):
                for k in range(NC):
                    last = three(ps[:, bank, :], w_hi[:, r, k, c * P:(c + 1) * P], w_lo[:, r, k, c * P:(c + 1) * P],
                                 t_hi[:, k, :], t_lo[:, k, :], k == 0, k == NC - 1)
                last.then_inc(s, 1)

            def a_sums(b):
                pe.wait_ge(kacc, b * NT + NT + FREE_ACC)
                a = ps[:, SMALL_BANK, :]
                one, plus, minus = half[:, 0:1], half[:, 1:2], half[:, 2:3]
                blk = [acc[:, i * P:(i + 1) * P] for i in range(NC + 2)]
                for dst, terms in ((0, ((0, plus), (1, plus), (4, plus), (5, plus))),
                                   (1, ((0, plus), (1, plus), (4, minus), (5, minus))),
                                   (2, ((2, one),)), (3, ((3, one),))):
                    for i, (m, vec) in enumerate(terms):
                        last = mm(a[:, dst:dst + 1], blk[m], vec, start=(i == 0), stop=(i == len(terms) - 1))
                last.then_inc(a_ps, 1)

            def attention(b, last):
                for t in range(NT):
                    kv_tile(b, t)
                for c in range(NC):
                    if c == 2:
                        a_sums(b)
                        pe.wait_ge(kv_sb, b * NT + 3)
                    if c == 0:
                        pe.wait_ge(t_los, b * NC + NC)
                        pe.wait_ge(o_y, b * NT + FREE_O)
                    feature_chunk(Q_BANKS[c], WQ, c, q_ps)
                for c in range(NC):
                    pe.wait_ge(q_los, b * NC + c + 1)
                    for t in range(NT):
                        if c == 0 and t == 0:
                            pe.wait_ge(kv_sb, b * NT + NT)
                        if c == 0 and t == 3:
                            pe.wait_ge(q_los, b * NC + 2)
                        done = three(ps[:, O_BANKS[t], :], g_hi[:, c, t * P:(t + 1) * P], g_lo[:, c, t * P:(t + 1) * P],
                                     w_hi[:, WO, c, :], w_lo[:, WO, c, :], c == 0, c == NC - 1)
                        if c == NC - 1:
                            done.then_inc(o_ps, 1)
                    if c == 0:
                        transposes(b + 1, 0)
                        transposes(b + 1, 1)
                    elif c < NC - 1:
                        transposes(b + 1, c + 1)

            pe.wait_ge(c_steps, 3)
            mod_row(0, xs[:, 2 * NT * D:3 * NT * D], wm_in[1])
            mod_row(1, xs[:, 3 * NT * D:4 * NT * D], wm_in[0])
            mod_row(2, xs[:, NT * D:2 * NT * D], wm_in[2])
            pe.wait_ge(const_in, N_CONST)
            for c in range(NC):
                transposes(0, c)
            weights_ready(3)
            pe.wait_ge(mod_sb, 7)
            with pe.Fori(0, B - 1) as b:
                attention(b, False)
            mod_col(0, stage[:, 0, :], wm_in[4])
            mod_col(1, stage[:, 1, :], wm_in[3])
            pe.wait_ge(mod_sb, 9)
            attention(B - 1, True)
            pe.wait_ge(t_full, (B + 1) * NC)
            mod_row(6, stage[:, 0, :], wm_in[5])

            def ffn(b, last):
                for c in range(NC):
                    pe.wait_ge(t_los, (b + B) * NC + c + 1) if c == NC - 1 else None
                for t in range(NT):
                    dst = ps[:, SMALL_BANK, t * 2 * NE:(t + 1) * 2 * NE]
                    for k in range(NC):
                        mm(dst, t_hi[:, k, t * P:(t + 1) * P], wg_r[:, k, :], start=(k == 0), stop=False)
                        done = mm(dst[:, 0:NE], t_lo[:, k, t * P:(t + 1) * P], wg_r[:, k, 0:NE],
                                  start=False, stop=(k == NC - 1))
                done.then_inc(lg_ps, 1)
                if isinstance(b, int):
                    pass
                for c in range(NC):
                    if c < 2:
                        pe.wait_ge(d_y, (b * NT + c - 2) * 2 + 1 + FREE_DY)
                    else:
                        pe.wait_ge(u_los, b * NC + c - 1)
                    feature_chunk(U_BANKS[c % 2], WUP, c, u_ps)
                for t in range(NT):
                    for k in range(NC):
                        done = three(ps[:, E_BANKS[t], :], t_hi[:, k, t * P:(t + 1) * P], t_lo[:, k, t * P:(t + 1) * P],
                                     w_hi[:, WEXP, k, :], w_lo[:, WEXP, k, :], k == 0, k == NC - 1)
                    done.then_inc(e_ps, 1)
                if not last:
                    pe.wait_ge(lg_s, b * 2 + 1)
                    transposes(b + B + 1, 0)
                    transposes(b + B + 1, 1)
                for t in range(NT):
                    if t < 2:
                        pe.wait_ge(u_los, b * NC + NC)
                    else:
                        pe.wait_ge(d_y, (b * NT + t - 2) * 2 + 1 + FREE_DY)
                    for k in range(NC):
                        done = three(ps[:, D_BANKS[t % 2], :], g_hi[:, k, t * P:(t + 1) * P], g_lo[:, k, t * P:(t + 1) * P],
                                     w_hi[:, WDOWN, k, :], w_lo[:, WDOWN, k, :], k == 0, k == NC - 1)
                    done.then_inc(d_ps, 1)
                    if t == 0 and not last:
                        transposes(b + B + 1, 2)
                        transposes(b + B + 1, 3)

            weights_ready(6)
            pe.wait_ge(x2_s, B * NT)
            with pe.Fori(0, B - 1) as b:
                ffn(b, False)
            ffn(B - 1, True)


def layout(inputs):
    import numpy as np
    a = {k: np.asarray(v) for k, v in inputs.items()}
    half_rot = D // 4
    perm = np.concatenate([np.arange(0, 2 * half_rot, 2), np.arange(1, 2 * half_rot, 2), np.arange(2 * half_rot, D)])

    def chunks(m):
        return np.ascontiguousarray(m.reshape(NC, P, -1).transpose(1, 0, 2).reshape(P, -1))

    w_in = a["L0_attn_W_in"].reshape(D, 3, D)[:, :, perm]
    b_in = a["L0_attn_b_in"].reshape(3, D)[:, perm]
    w = [w_in[:, 1], w_in[:, 2], w_in[:, 0], a["L0_attn_W_out"][perm, :],
         a["L0_ffn_W_up"].T, a["L0_ffn_W_expert"], a["L0_ffn_W_down"].T]
    wmod = a["L0_wmod"].reshape(D, NCOMP, D)
    cols = [chunks(v.reshape(D, 1)) for v in (a["L0_attn_gamma"], a["L0_attn_beta"], b_in[0])]
    cols += [chunks(a["L0_c"].T), chunks(a["L0_ffn_W_gate"].T)]
    rot_dim = D // 2
    inv = (1.0 / 10000.0 ** (np.arange(0, rot_dim, 2, dtype=np.float32) / np.float32(rot_dim))).astype(np.float32)
    ang = (np.arange(S, dtype=np.float32)[:, None] * inv[None, :]).astype(np.float64)
    rot = np.concatenate([np.cos(2 * ang), -np.sin(2 * ang)], axis=1).astype(np.float32)
    return {
        "X": np.ascontiguousarray(a["L0_attn_X"]),
        "cols": np.ascontiguousarray(np.concatenate(cols, axis=1)),
        "ident": np.eye(P, dtype=np.float32),
        "rot": np.ascontiguousarray(rot.reshape(NT, P, -1).transpose(1, 0, 2)),
        "w": np.stack([chunks(m) for m in w]),
        "wmod": np.stack([chunks(wmod[:, i]) for i in range(NCOMP)]),
        "brow": np.ascontiguousarray(np.concatenate([b_in[1], b_in[2], a["L0_attn_b_out"]])[None, :]),
    }


def kernel(**inputs):
    import numpy as np
    import concourse.bacc as bacc
    from concourse.bass_utils import run_bass_kernel_spmd

    arrays = layout(inputs)
    nc = bacc.Bacc("TRN2", target_bir_lowering=False, num_devices=1, dynamic_dma_scratch_size=8192)
    args = {k: nc.dram_tensor(f"in_{k}", v.shape, mybir.dt.from_np(v.dtype), kind="ExternalInput").ap()
            for k, v in arrays.items()}
    out = nc.dram_tensor("out_0", (B, S, D), mybir.dt.float32, kind="ExternalOutput").ap()
    build(nc, **args, out=out)
    r = run_bass_kernel_spmd(nc, [{f"in_{k}": v for k, v in arrays.items()}], core_ids=[0])
    return r.results[0]["out_0"]
```

```python
import concourse.bass as bass
from concourse import mybir
from contextlib import ExitStack

P = 128
B, S, D = 4, 512, 512
NT = S // P
NC = D // P
ROT = D // 4
NE = 8
NCOMP = 6
EPS = 1e-5
MIN_GATE = 0.25
IDENTITY_WEIGHT = 0.5

COL_GAMMA, COL_BETA, COL_BQ, COL_C, COL_WG = 0, NC, 2 * NC, 3 * NC, 3 * NC + NC * B
COLS = COL_WG + NC * NE

WK, WV, WQ, WO = range(4)
WUP, WEXP, WDOWN = WK, WV, WQ

KV_BANKS = ((0, 1), (2, 3))
Q_BANKS = (4, 5, 0, 1)
O_BANKS = (2, 3, 4, 5)
U_BANKS = (4, 5)
E_BANKS = (0, 1, 2, 3)
D_BANKS = (4, 5)
T_BANKS = (6, 7)
SMALL_BANK = 7


def build(nc, X, cols, ident, rot, w, wmod, brow, out):
    f32 = mybir.dt.float32
    f32r = mybir.dt.float32r
    ALU = mybir.AluOpType
    ACT = mybir.ActivationFunctionType

    x_rows = X.rearrange("b (t p) d -> (b t) p d", p=P)
    out_rows = out.rearrange("b (t p) d -> (b t) p d", p=P)
    x_batch = X.rearrange("b (t p) d -> b p t d", p=P)
    out_batch = out.rearrange("b (t p) d -> b p t d", p=P)
    ROW_CA, ROW_SA, ROW_GA, ROW_GB = range(4)
    mod_rows = nc.dram_tensor("mod_rows", (4, B, D), f32, kind="Internal").ap()

    ctx = ExitStack()
    with ctx:
        def sb(name, shape, dt=f32):
            return ctx.enter_context(nc.sbuf_tensor(name, shape, dt))

        def sem(name):
            return ctx.enter_context(nc.semaphore(name))

        w_hi = sb("w_hi", [P, 4, NC, D], f32r)
        w_lo = sb("w_lo", [P, 4, NC, D], f32r)
        wg_r = sb("wg_r", [P, NC, 2 * NE], f32r)
        stage = sb("stage", [P, 2, NC * D])
        t_hi = sb("t_hi", [P, NC, S], f32r)
        t_lo = sb("t_lo", [P, NC, S], f32r)
        g_hi = sb("g_hi", [P, NC, S], f32r)
        g_lo = sb("g_lo", [P, NC, S], f32r)
        xs = sb("xs", [P, B * NT * D])
        h1 = sb("h1", [P, NT * D])
        z = sb("z", [P, NT, D])
        ca_bc = sb("ca_bc", [P, D])
        sa_bc = sb("sa_bc", [P, D])
        gate_bc = sb("gate_bc", [P, B * D])
        bkv_bc = sb("bkv_bc", [P, 2, D])
        bo_bc = sb("bo_bc", [P, D])
        rot_sb = sb("rot_sb", [P, NT, 2 * ROT])
        kv = sb("kv", [P, 2, 2, D])
        prod = sb("prod", [P, D + 2 * ROT])
        cross = sb("cross", [P, 2 * ROT])
        acc = sb("acc", [P, D + 2 * ROT])
        full = sb("full", [P, 2, S])
        tmp = sb("tmp", [P, 2, D])
        es = kv[:, :, 0, :]
        rows = kv[0:B, :, 0, :]
        gate_rows = tmp[0:B]
        sign = kv[0:B, :, 1, :]
        col = sb("col", [P, COLS])
        idn = sb("idn", [P, P])
        half = sb("half", [P, 2])
        ones = sb("ones", [1, P])
        xnm = sb("xnm", [P, NT])
        fold = sb("fold", [P, 2, ROT])
        pair = sb("pair", [P, 2, ROT])
        expo = sb("expo", [P, NT])
        sc = sb("sc", [P, NC * B])
        sc_t = sb("sc_t", [P, 3, NC * B])
        cb_col = sb("cb_col", [P, B * NC])
        sb_col = sb("sb_col", [P, B * NC])
        xst = sb("xst", [P, NT, 6])
        xmv = sb("xmv", [P, NT, 2])
        xve = sb("xve", [P, NT])
        xrs = sb("xrs", [P, NT])
        hst = sb("hst", [P, NT, 6])
        hmv = sb("hmv", [P, NT, 2])
        hve = sb("hve", [P, NT])
        hrs = sb("hrs", [P, NT])
        hnm = sb("hnm", [P, NT])
        nsq = sb("nsq", [P, 2, 2])
        rnm = sb("rnm", [P, 2, 2])
        wgt = sb("wgt", [P, 2])
        sqj = sb("sqj", [P, D], mybir.dt.bfloat16)
        a_col = sb("a_col", [P, NC])
        ab_col = sb("ab_col", [P, NC])
        lgt = sb("lgt", [2 * NE, S])
        lg2 = sb("lg2", [P, NT, 2 * NE])
        lg = sb("lg", [P, NT, NE])
        top8 = sb("top8", [P, NT, 8])
        tdif = sb("tdif", [P, NT, 2])
        tex = sb("tex", [P, NT, 2])
        tsum = sb("tsum", [P, NT])
        trec = sb("trec", [P, NT])
        trw = sb("trw", [P, NT, 2])
        rsum = sb("rsum", [P, NT])
        ps = ctx.enter_context(nc.psum_tensor("ps", [P, 8, 512], f32))

        col_in = sem("col_in")
        const_in = sem("const_in")
        x_in = sem("x_in")
        wm_in = [sem(f"wm_in{i}") for i in range(NCOMP)]
        ca_w = [sem(f"ca_w{k}") for k in range(NC)]
        sa_w = [sem(f"sa_w{k}") for k in range(NC)]
        w_in = [sem(f"w_in{i}") for i in range(7)]
        row_out = sem("row_out")
        ca_in = sem("ca_in")
        ga_in = sem("ga_in")
        gb_in = sem("gb_in")
        waits_done = sem("waits_done")
        cst = sem("cst")
        c_exp = sem("c_exp")
        c_steps = sem("c_steps")
        wg_hi_s = sem("wg_hi_s")
        mod_ps = sem("mod_ps")
        mod_sb = sem("mod_sb")
        whi = sem("whi")
        wlo = sem("wlo")
        wlo_k, wlo_v = sem("wlo_k"), sem("wlo_v")
        ident_in = sem("ident_in")
        gate_out = sem("gate_out")
        lg_t = sem("lg_t")
        lg_ps2 = sem("lg_ps2")
        bc_ps, bc_s = sem("bc_ps"), sem("bc_s")
        afold = sem("afold")
        xst_s, xmv_s, xve_s, xrs_s = (sem(n) for n in ("xst_s", "xmv_s", "xve_s", "xrs_s"))
        xnm_s = sem("xnm_s")
        xn_s = sem("xn_s")
        scaled0_s = sem("scaled0_s")
        scaled_s = sem("scaled_s")
        h1_s = sem("h1_s")
        hst_s, hmv_s, hve_s, hrs_s, hnm_s = (sem(n) for n in ("hst_s", "hmv_s", "hve_s", "hrs_s", "hnm_s"))
        z_s = sem("z_s")
        t_ps, t_full, t_his, t_los = (sem(n) for n in ("t_ps", "t_full", "t_his", "t_los"))
        r_s = sem("r_s")
        kv_ps, kv_sb = sem("kv_ps"), sem("kv_sb")
        nsq_s, rnm_s, wgt_s = sem("nsq_s"), sem("rnm_s"), sem("wgt_s")
        kprod, kcross, krot, kacc = (sem(n) for n in ("kprod", "kcross", "krot", "kacc"))
        a_ps, a_sb, ab_sb = sem("a_ps"), sem("a_sb"), sem("ab_sb")
        q_ps, q_full, q_his, q_los = (sem(n) for n in ("q_ps", "q_full", "q_his", "q_los"))
        o_ps, o_y, x2_s = sem("o_ps"), sem("o_y"), sem("x2_s")
        lg_ps, lg_s, top_s, ex_s, rsum_s = (sem(n) for n in ("lg_ps", "lg_s", "top_s", "ex_s", "rsum_s"))
        lg_sum = sem("lg_sum")
        u_ps, u_his, u_los = (sem(n) for n in ("u_ps", "u_his", "u_los"))
        e_ps, es_s = sem("e_ps"), sem("es_s")
        d_ps, d_y, out_s = sem("d_ps"), sem("d_y"), sem("out_s")
        out_dma = sem("out_dma")

        block = ctx.enter_context(nc.Block())

        FREE_NSQ, FREE_RNM, FREE_ACC, FREE_O, FREE_DY = 4, 2, 1, NT, 4

        def wait(eng, s, v):
            if not (isinstance(v, int) and v <= 0):
                eng.wait_ge(s, v)

        def tok(b, t):
            return bass.ds((b * NT + t) * D, D)

        def x_slot(b):
            return xs[:, b * NT * D:(b + 1) * NT * D]

        def wait_apart(eng, s, v):
            eng.wait_ge(s, v)
            eng.sem_inc(waits_done, 1)

        N_CONST = 3 * 16
        W_ORDER = (WK, WV, WQ, WO, WUP, WEXP, WDOWN)

        w_raw = (stage[:, 0, :], stage[:, 1, :], x_slot(1), stage[:, 0, :], stage[:, 1, :], stage[:, 0, :], stage[:, 1, :])

        @block.sync
        def _(sp):
            sp.dma_start(col[:], cols).then_inc(col_in, 16)
            for k in range(NC):
                sp.dma_start(x_slot(2)[:, k * D:(k + 1) * D], wmod[1][:, k * D:(k + 1) * D]).then_inc(ca_w[k], 16)
            sp.dma_start(x_slot(0).rearrange("p (t d) -> p t d", t=NT), x_batch[0]).then_inc(x_in, 16)
            for k in range(NC):
                sp.dma_start(x_slot(3)[:, k * D:(k + 1) * D], wmod[0][:, k * D:(k + 1) * D]).then_inc(sa_w[k], 16)
            sp.dma_start(x_slot(1), wmod[2]).then_inc(wm_in[2], 16)
            sp.dma_start(gate_bc[:], wmod[4]).then_inc(wm_in[4], 16)
            sp.dma_start(idn[:], ident).then_inc(ident_in, 16)
            sp.wait_ge(mod_ps, 1)
            sp.dma_start(x_slot(2), wmod[5]).then_inc(wm_in[5], 16)
            sp.wait_ge(mod_ps, 2)
            sp.dma_start(x_slot(3), wmod[3]).then_inc(wm_in[3], 16)
            sp.dma_start(w_raw[0], w[0]).then_inc(w_in[0], 16)
            sp.dma_start(w_raw[1], w[1]).then_inc(w_in[1], 16)
            sp.wait_ge(mod_sb, 2)
            sp.dma_start(mod_rows[ROW_CA], rows[:, 0, :]).then_inc(row_out, 16)
            sp.dma_start(mod_rows[ROW_SA], rows[:, 1, :]).then_inc(row_out, 16)
            sp.dma_start(bkv_bc[:].rearrange("p a d -> p (a d)"), brow[0:1, 0:2 * D].to_broadcast([P, 2 * D])).then_inc(const_in, 16)
            sp.dma_start(rot_sb[:], rot).then_inc(const_in, 16)
            sp.dma_start(bo_bc[:], brow[0:1, 2 * D:3 * D].to_broadcast([P, D])).then_inc(const_in, 16)
            sp.wait_ge(mod_ps, 3)
            sp.dma_start(w_raw[2], w[2]).then_inc(w_in[2], 16)
            sp.wait_ge(mod_sb, 8)
            sp.dma_start(mod_rows[ROW_GA], gate_rows[:, 0, :]).then_inc(gate_out, 16)
            sp.dma_start(mod_rows[ROW_GB], gate_rows[:, 1, :]).then_inc(gate_out, 16)
            sp.wait_ge(gate_out, 32)
            for b in range(B):
                sp.dma_start(gate_bc[:, b * D:(b + 1) * D],
                             mod_rows[ROW_GA, b:b + 1, :].to_broadcast([P, D])).then_inc(ga_in, 16)
            sp.wait_ge(row_out, 32)
            sp.wait_ge(wlo_k, NC)
            sp.dma_start(w_raw[3], w[3]).then_inc(w_in[3], 16)
            sp.wait_ge(wlo_v, NC)
            sp.dma_start(w_raw[4], w[4]).then_inc(w_in[4], 16)
            sp.wait_ge(mod_ps, 6)
            sp.wait_ge(wlo, 1)

            with sp.Fori(0, B - 1) as b:
                sp.wait_ge(x_in, b * 16 + 16)
                sp.dma_start(xs[:, bass.ds((b + 1) * NT * D, NT * D)].rearrange("p (t d) -> p t d", t=NT),
                             x_batch[bass.ds(b + 1, 1)].rearrange("o p t d -> (o p) t d")).then_inc(x_in, 16)
                sp.wait_ge(h1_s, b * NT + NT)
                sp.dma_start(ca_bc[:], mod_rows[ROW_CA, bass.ds(b + 1, 1), :].to_broadcast([P, D])).then_inc(ca_in, 16)
                sp.dma_start(sa_bc[:], mod_rows[ROW_SA, bass.ds(b + 1, 1), :].to_broadcast([P, D])).then_inc(ca_in, 16)
            sp.wait_ge(wlo, 2)
            sp.dma_start(w_raw[5], w[5]).then_inc(w_in[5], 16)
            sp.wait_ge(wlo, 3)
            sp.dma_start(w_raw[6], w[6]).then_inc(w_in[6], 16)
            sp.wait_ge(o_y, B * NT + FREE_O)
            for b in range(B):
                sp.dma_start(gate_bc[:, b * D:(b + 1) * D],
                             mod_rows[ROW_GB, b:b + 1, :].to_broadcast([P, D])).then_inc(gb_in, 16)
            with sp.Fori(0, B * NT) as i:
                sp.wait_ge(out_s, i + 1)
                sp.dma_start(out_rows[bass.ds(i, 1)].rearrange("o p d -> (o p) d"),
                             xs[:, bass.ds(i * D, D)]).then_inc(out_dma, 16)
            sp.wait_ge(out_dma, B * NT * 16)

        @block.gpsimd
        def _(pool):
            def power(dst, src, n, s):
                nc.gpsimd.tensor_tensor(dst, src, expo[:, 0:n], ALU.pow).then_inc(s, 1)

            def rstd_x(g):
                pool.wait_ge(xve_s, g + 1)
                power(xrs[:], xve[:], NT, xrs_s)

            def rstd_h(g, t0, n):
                pool.wait_ge(hve_s, g * NT + t0 + n)
                wait(pool, z_s, g * NT)
                nc.gpsimd.tensor_tensor(hrs[:, t0:t0 + n], hve[:, t0:t0 + n], expo[:, 0:n], ALU.pow).then_inc(hrs_s, n)

            def low_k(k):
                nc.gpsimd.tensor_tensor(w_lo[:, WK, k, :], w_raw[0][:, k * D:(k + 1) * D],
                                        w_hi[:, WK, k, :].bitcast(f32), ALU.subtract).then_inc(wlo_k, 1)

            def weight(b, t):
                pool.wait_ge(nsq_s, (b * NT + t) * 2 + 2 + FREE_NSQ)
                power(rnm[:, t % 2, :], nsq[:, t % 2, :], 2, rnm_s)
                pool.wait_ge(rnm_s, b * NT + t + 1 + FREE_RNM)
                nc.gpsimd.tensor_tensor(wgt[:, t % 2:t % 2 + 1], rnm[:, t % 2, 0:1], rnm[:, t % 2, 1:2],
                                        ALU.mult).then_inc(wgt_s, 1)

            def residual(g, t):
                base = (g * NT + t) * 3
                h = h1[:, t * D:(t + 1) * D]
                pool.wait_ge(z_s, g * NT + t + 1)
                nc.gpsimd.tensor_tensor(h, h, bo_bc[:], ALU.add).then_inc(r_s, 1)
                wait_apart(pool, r_s, base + 1)
                nc.gpsimd.tensor_tensor(h, h, gate_bc[:, bass.ds(g * D, D)], ALU.mult).then_inc(r_s, 1)
                wait_apart(pool, r_s, base + 2)
                nc.gpsimd.tensor_tensor(xs[:, tok(g, t)], xs[:, tok(g, t)], h, ALU.add).then_inc(r_s, 1)

            def attention_out(b, t):
                wait_apart(pool, o_y, b * NT + t + 1 + FREE_O)
                if t == 0:
                    wait_apart(pool, r_s, (b * NT + NT) * 3)
                nc.gpsimd.tensor_tensor(xs[:, tok(b, t)], xs[:, tok(b, t)], tmp[:, t % 2, :], ALU.add).then_inc(x2_s, 1)

            def scale_rows(g, t):
                pool.wait_ge(xn_s, g * NT + t + 1)
                pool.wait_ge(r_s, ((g - 1) * NT + t + 1) * 3)
                if t == 0:
                    pool.wait_ge(ca_in, g * 32)
                nc.gpsimd.tensor_tensor(h1[:, t * D:(t + 1) * D], z[:, t, :], ca_bc[:], ALU.mult).then_inc(scaled_s, 1)

            def attention(b, last):
                weight(b, 0)
                residual(b, 1)
                weight(b, 1)
                rstd_h(b + 1, 0, NT) if last else rstd_x(b + 1)
                residual(b, 2)
                weight(b, 2)
                if not last:
                    for t in range(3):
                        scale_rows(b + 1, t)
                weight(b, 3)
                residual(b, 3)
                if not last:
                    scale_rows(b + 1, 3)
                    rstd_h(b + 1, 0, 2)
                    rstd_h(b + 1, 2, 2)
                    residual(b + 1, 0)
                for t in range(NT):
                    attention_out(b, t)

            pool.sem_inc(rnm_s, FREE_RNM)
            pool.wait_ge(cst, 4)
            rstd_x(0)
            rstd_h(0, 0, 2)
            rstd_h(0, 2, 2)
            pool.wait_ge(whi, 1)
            for k in range(NC):
                low_k(k)
            pool.wait_ge(ga_in, B * 16)
            pool.wait_ge(const_in, N_CONST)
            residual(0, 0)
            with pool.Fori(0, B - 1) as b:
                attention(b, False)
            attention(B - 1, True)

            def ffn_out(b, t):
                n = b * NT + t
                wait_apart(pool, d_y, n * 2 + 2 + FREE_DY)
                nc.gpsimd.tensor_tensor(xs[:, tok(b, t)], xs[:, tok(b, t)], tmp[:, t % 2, :], ALU.add).then_inc(out_s, 1)

            with pool.Fori(0, B - 1) as b:
                rstd_h(b + B + 1, 0, NT)
                for t in range(NT):
                    ffn_out(b, t)
            for t in range(NT):
                ffn_out(B - 1, t)

        @block.scalar
        def _(act):
            def split_hi(i):
                act.wait_ge(w_in[i], 16)
                if i == 4:
                    act.wait_ge(kv_ps, B * NT)
                if i == 6:
                    act.wait_ge(q_ps, B * NC)
                nc.scalar.activation(w_hi[:, W_ORDER[i]].rearrange("p k n -> p (k n)"), w_raw[i], ACT.Copy).then_inc(whi, 1)

            def norm_sums(b, t):
                act.wait_ge(kv_sb, b * NT + t + 1)
                act.wait_ge(rnm_s, b * NT + t - 1 + FREE_RNM)
                for i in range(2):
                    act.wait_ge(nsq_s, (b * NT + t) * 2 + i + FREE_NSQ)
                    nc.scalar.activation(sqj[:], kv[:, t % 2, i, :], ACT.Square,
                                         accum_out=nsq[:, t % 2, i:i + 1]).then_inc(nsq_s, 1)

            def normalise_x(g):
                act.wait_ge(xnm_s, g + 1)
                wait(act, t_ps, g * NC)
                for t in range(NT):
                    nc.scalar.activation(z[:, t, :], xs[:, tok(g, t)], ACT.Identity, bias=xnm[:, t:t + 1],
                                         scale=xrs[:, t:t + 1]).then_inc(xn_s, 1)

            def normalise(g, t0, n):
                act.wait_ge(hnm_s, g * NT + t0 + n)
                if t0 == 0:
                    wait(act, t_ps, g * NC)
                for t in range(t0, t0 + n):
                    src = h1[:, t * D:(t + 1) * D] if first_ln(g) else xs[:, tok(g_off(g), t)]
                    nc.scalar.activation(z[:, t, :], src, ACT.Identity, bias=hnm[:, t:t + 1],
                                         scale=hrs[:, t:t + 1]).then_inc(z_s, 1)

            def t_evac(g, c, ffn, after_q=False):
                n = g * NC + c
                act.wait_ge(t_ps, n + 1)
                if after_q and c < 2:
                    act.wait_ge(q_los, n - 1)
                else:
                    wait(act, t_los, n - 1)
                if ffn:
                    j = bass.ds((g - B) * NC + c, 1)
                    scale, bias = cb_col[:, j], sb_col[:, j]
                else:
                    scale, bias = col[:, COL_GAMMA + c:COL_GAMMA + c + 1], col[:, COL_BETA + c:COL_BETA + c + 1]
                nc.scalar.activation(full[:, c % 2, :], ps[:, T_BANKS[c % 2], :], ACT.Identity,
                                     bias=bias, scale=scale).then_inc(t_full, 1)
                act.wait_ge(t_full, n + 1)
                nc.scalar.activation(t_hi[:, c, :], full[:, c % 2, :], ACT.Copy).then_inc(t_his, 1)

            def q_evac(b, c):
                n = b * NC + c
                act.wait_ge(q_ps, n + 1)
                if c == 0:
                    act.wait_ge(ab_sb, b + 1)
                if c >= 2:
                    act.wait_ge(q_los, n - 1)
                else:
                    act.wait_ge(t_los, n + 3)
                nc.scalar.activation(full[:, c % 2, :], ps[:, Q_BANKS[c], :], ACT.Identity,
                                     bias=ab_col[:, c:c + 1], scale=a_col[:, c:c + 1]).then_inc(q_full, 1)
                act.wait_ge(q_full, n + 1)
                nc.scalar.activation(g_hi[:, c, :], full[:, c % 2, :], ACT.Copy).then_inc(q_his, 1)

            def u_evac(b, c):
                act.wait_ge(u_ps, b * NC + c + 1)
                nc.scalar.activation(g_hi[:, c, :], ps[:, U_BANKS[c % 2], :], ACT.Relu).then_inc(u_his, 1)

            def e_evac(b, t):
                act.wait_ge(e_ps, b * NT + t + 1)
                if t == 0:
                    act.wait_ge(rsum_s, b + 1)
                act.wait_ge(d_y, (b * NT + t - 2) * 2 + 1 + FREE_DY)
                nc.scalar.activation(es[:, t % 2, :], ps[:, E_BANKS[t], :], ACT.Copy,
                                     scale=rsum[:, t:t + 1]).then_inc(es_s, 1)

            def attention(b, last):
                for t in range(NT):
                    norm_sums(b, t)
                    if t == 2 and not last:
                        normalise_x(b + 1)
                state["first"] = not last
                if last:
                    split_hi(4)
                    split_hi(5)
                    normalise(b + 1, 0, NT)
                for c in range(NC):
                    q_evac(b, c)
                if not last:
                    normalise(b + 1, 0, 2)
                    normalise(b + 1, 2, 2)
                for c in range(NC):
                    if c == 0:
                        act.wait_ge(q_ps, b * NC + NC)
                    t_evac(b + 1, c, last, after_q=True)

            state = {"first": True}

            def first_ln(g):
                return state["first"]

            def g_off(g):
                return g - B

            act.sem_inc(nsq_s, FREE_NSQ)
            act.wait_ge(col_in, 16)
            nc.scalar.activation(sc_t[:, 0, :], col[:, COL_C:COL_C + NC * B], ACT.Exp, scale=-1.0).then_inc(c_exp, 1)
            nc.scalar.activation(wg_r[:, :, 0:NE], col[:, COL_WG:COLS].rearrange("p (k e) -> p k e", k=NC),
                                 ACT.Copy).then_inc(wg_hi_s, 1)
            normalise_x(0)
            for i, dst in enumerate((ca_bc, sa_bc)):
                act.wait_ge(bc_ps, i + 1)
                nc.scalar.activation(dst[:], ps[:, 2 + i, :], ACT.Copy).then_inc(bc_s, 1)
            normalise(0, 0, 2)
            normalise(0, 2, 2)
            split_hi(0)
            for c in range(NC):
                t_evac(0, c, False)
            split_hi(1)
            split_hi(2)
            split_hi(3)
            act.wait_ge(mod_sb, 9)
            with act.Fori(0, B - 1) as b:
                attention(b, False)
            attention(B - 1, True)
            split_hi(6)

            def ffn(b, last):
                act.wait_ge(lg_ps, b + 1)
                nc.scalar.activation(lgt[:], ps[0:2 * NE, SMALL_BANK, :], ACT.Copy).then_inc(lg_t, 1)
                for c in range(NC):
                    u_evac(b, c)
                    if c == 1:
                        act.wait_ge(top_s, b * 5 + 5)
                        nc.scalar.activation(tex[:], tdif[:], ACT.Exp).then_inc(ex_s, 1)
                if not last:
                    normalise(b + B + 1, 0, NT)
                for c in range(NC):
                    if not last:
                        if c == 0:
                            act.wait_ge(e_ps, b * NT + NT)
                        t_evac(b + B + 1, c, True)
                    if c % 2 or last:
                        e_evac(b, c // 2 if not last else c)
                if not last:
                    e_evac(b, 2)
                    e_evac(b, 3)

            state["first"] = False
            with act.Fori(0, B - 1) as b:
                ffn(b, False)
            ffn(B - 1, True)

        @block.vector
        def _(dve):
            v = nc.vector

            def split_lo(i):
                dve.wait_ge(whi, i + 1)
                if i == 4:
                    dve.wait_ge(kv_ps, B * NT)
                r = W_ORDER[i]
                v.tensor_tensor(w_lo[:, r].rearrange("p k n -> p (k n)"), w_raw[i],
                                w_hi[:, r].rearrange("p k n -> p (k n)").bitcast(f32), ALU.subtract).then_inc(wlo, 1)

            def x_stats(g):
                dve.wait_ge(x_in, g * 16 + 16)
                for t in range(NT):
                    v.bn_stats(xst[:, t, :], xs[:, tok(g, t)]).then_inc(xst_s, 1)
                for t in range(NT):
                    wait_apart(dve, xst_s, g * NT + t + 1)
                    v.bn_aggr(xmv[:, t, :], xst[:, t, :]).then_inc(xmv_s, 1)
                dve.wait_ge(xmv_s, g * NT + NT)
                v.tensor_scalar(xve[:], xmv[:, :, 1], EPS, None, ALU.add).then_inc(xve_s, 1)

            def x_shift(g):
                dve.wait_ge(xrs_s, g + 1)
                v.scalar_tensor_tensor(xnm[:], xmv[:, :, 0], -1.0, xrs[:], ALU.mult, ALU.mult).then_inc(xnm_s, 1)

            def h_row(g, t):
                n = g * NT + t
                h = h1[:, t * D:(t + 1) * D]
                if isinstance(g, int):
                    dve.wait_ge(scaled0_s, t + 1)
                else:
                    dve.wait_ge(scaled_s, n + 1 - NT)
                v.tensor_tensor(h, h, sa_bc[:], ALU.add).then_inc(h1_s, 1)

            def h_stats(g, t):
                dve.wait_ge(h1_s, g * NT + t + 1)
                v.bn_stats(hst[:, t, :], h1[:, t * D:(t + 1) * D]).then_inc(hst_s, 1)

            def x2_rows(g, t):
                if t == 0:
                    wait_apart(dve, x2_s, (g - B + 1) * NT)
                v.bn_stats(hst[:, t, :], xs[:, tok(g - B, t)]).then_inc(hst_s, 1)

            def h_aggr(g, t0, n):
                for t in range(t0, t0 + n):
                    wait_apart(dve, hst_s, g * NT + t + 1)
                    v.bn_aggr(hmv[:, t, :], hst[:, t, :]).then_inc(hmv_s, 1)
                dve.wait_ge(hmv_s, g * NT + t0 + n)
                v.tensor_scalar(hve[:, t0:t0 + n], hmv[:, t0:t0 + n, 1], EPS, None, ALU.add).then_inc(hve_s, n)

            def h_shift(g, t0, n):
                dve.wait_ge(hrs_s, g * NT + t0 + n)
                v.scalar_tensor_tensor(hnm[:, t0:t0 + n], hmv[:, t0:t0 + n, 0], -1.0, hrs[:, t0:t0 + n],
                                       ALU.mult, ALU.mult).then_inc(hnm_s, n)

            def t_split(g, c):
                dve.wait_ge(t_his, g * NC + c + 1)
                v.tensor_tensor(t_lo[:, c, :], full[:, c % 2, :], t_hi[:, c, :].bitcast(f32),
                                ALU.subtract).then_inc(t_los, 1)

            def kv_rows(b, t):
                n = b * NT + t
                pair = KV_BANKS[t % 2]
                dve.wait_ge(kv_ps, n + 1)
                dve.wait_ge(nsq_s, (n - 1) * 2 + FREE_NSQ)
                v.tensor_tensor(kv[:, t % 2], ps[:, pair[0]:pair[0] + 2, :], bkv_bc[:], ALU.add).then_inc(kv_sb, 1)

            def kv_products(b, t):
                n = b * NT + t
                k, val = kv[:, t % 2, 0, :], kv[:, t % 2, 1, :]
                dve.wait_ge(kv_sb, n + 1)
                v.tensor_tensor(cross[:, 0:ROT], k[:, 0:ROT], val[:, ROT:2 * ROT], ALU.mult).then_inc(kcross, 1)
                v.tensor_tensor(cross[:, ROT:2 * ROT], k[:, ROT:2 * ROT], val[:, 0:ROT], ALU.mult).then_inc(kcross, 1)
                dve.wait_ge(kacc, n + FREE_ACC)
                v.tensor_tensor(prod[:, 0:D], k, val, ALU.mult).then_inc(kprod, 1)
                dve.wait_ge(kcross, n * 2 + 2)
                v.tensor_tensor(prod[:, D + ROT:D + 2 * ROT], cross[:, 0:ROT], cross[:, ROT:2 * ROT],
                                ALU.add).then_inc(krot, 1)
                dve.wait_ge(kprod, n + 1)
                v.tensor_tensor(prod[:, D:D + ROT], prod[:, 0:ROT], prod[:, ROT:2 * ROT], ALU.subtract).then_inc(krot, 1)
                dve.wait_ge(krot, n * 3 + 2)
                v.tensor_tensor(prod[:, D:D + 2 * ROT], prod[:, D:D + 2 * ROT], rot_sb[:, t, :],
                                ALU.mult).then_inc(krot, 1)

            def kv_sum(b, t):
                n = b * NT + t
                dve.wait_ge(krot, n * 3 + 3)
                dve.wait_ge(wgt_s, n + 1)
                if t == 0:
                    v.tensor_scalar(acc[:], prod[:], wgt[:, 0:1], None, ALU.mult).then_inc(kacc, 1)
                else:
                    dve.wait_ge(kacc, n + FREE_ACC)
                    v.scalar_tensor_tensor(acc[:], prod[:], wgt[:, t % 2:t % 2 + 1], acc[:],
                                           ALU.mult, ALU.add).then_inc(kacc, 1)

            def a_pairs(b):
                dve.wait_ge(kacc, b * NT + NT + FREE_ACC)
                blocks = acc[:].rearrange("p (g i r) -> p g i r", g=3, i=2)
                v.tensor_tensor(fold[:], blocks[:, 0:3:2, 0, :], blocks[:, 0:3:2, 1, :], ALU.add).then_inc(afold, 1)
                dve.wait_ge(afold, b * 3 + 1)
                v.tensor_tensor(pair[:, 0, :], fold[:, 0, :], fold[:, 1, :], ALU.add).then_inc(afold, 1)
                v.tensor_tensor(pair[:, 1, :], fold[:, 0, :], fold[:, 1, :], ALU.subtract).then_inc(afold, 1)

            def a_evac(b):
                dve.wait_ge(a_ps, b + 1)
                v.tensor_scalar(a_col[:], ps[:, SMALL_BANK, 0:NC], 1.0 - IDENTITY_WEIGHT, IDENTITY_WEIGHT,
                                ALU.mult, ALU.add).then_inc(a_sb, 1)
                dve.wait_ge(a_sb, b + 1)
                v.tensor_tensor(ab_col[:], a_col[:], col[:, COL_BQ:COL_BQ + NC], ALU.mult).then_inc(ab_sb, 1)

            def q_split(b, c):
                dve.wait_ge(q_his, b * NC + c + 1)
                v.tensor_tensor(g_lo[:, c, :], full[:, c % 2, :], g_hi[:, c, :].bitcast(f32),
                                ALU.subtract).then_inc(q_los, 1)

            def o_evac(b, t):
                n = b * NT + t
                dve.wait_ge(o_ps, n + 1)
                if t >= 2:
                    dve.wait_ge(x2_s, n - 1)
                v.tensor_tensor(tmp[:, t % 2, :], ps[:, O_BANKS[t], :], gate_bc[:, bass.ds(b * D, D)],
                                ALU.mult).then_inc(o_y, 1)

            def attention(b, last):
                for t in range(NT):
                    kv_rows(b, t)
                    if t > 0:
                        kv_sum(b, t - 1)
                    kv_products(b, t)
                    if t == 0 and not last:
                        x_stats(b + 1)
                    elif t == 0:
                        for j in range(NT):
                            x2_rows(B, j)
                        h_aggr(B, 0, NT)
                    elif t == 1 and not last:
                        x_shift(b + 1)
                    elif t == 1:
                        h_shift(B, 0, NT)
                kv_sum(b, NT - 1)
                a_pairs(b)
                if last:
                    split_lo(4)
                    a_evac(b)
                    q_split(b, 0)
                    q_split(b, 1)
                    split_lo(5)
                    q_split(b, 2)
                    q_split(b, 3)
                else:
                    dve.wait_ge(ca_in, b * 32 + 32)
                    h_row(b + 1, 0)
                    h_row(b + 1, 1)
                    a_evac(b)
                    h_stats(b + 1, 0)
                    h_stats(b + 1, 1)
                    q_split(b, 0)
                    h_aggr(b + 1, 0, 2)
                    h_row(b + 1, 2)
                    q_split(b, 1)
                    h_shift(b + 1, 0, 2)
                    h_row(b + 1, 3)
                    h_stats(b + 1, 2)
                    q_split(b, 2)
                    h_stats(b + 1, 3)
                    h_aggr(b + 1, 2, 2)
                    q_split(b, 3)
                    h_shift(b + 1, 2, 2)
                for c in range(NC):
                    t_split(b + 1, c)
                for t in range(NT):
                    o_evac(b, t)

            def guard_gates(done):
                g = gate_rows
                v.tensor_copy(g, ps[0:B, 4:6, :]).then_inc(mod_sb, 1)
                dve.wait_ge(mod_sb, done + 1)
                v.tensor_scalar(sign, g, 0.0, 2.0, ALU.is_ge, ALU.mult).then_inc(mod_sb, 1)
                dve.wait_ge(mod_sb, done + 2)
                v.scalar_tensor_tensor(g, g, -1.0, g, ALU.mult, ALU.max).then_inc(mod_sb, 1)
                dve.wait_ge(mod_sb, done + 3)
                v.tensor_scalar(g, g, MIN_GATE, None, ALU.max).then_inc(mod_sb, 1)
                dve.wait_ge(mod_sb, done + 4)
                v.scalar_tensor_tensor(g, sign, -1.0, g, ALU.add, ALU.mult).then_inc(mod_sb, 1)

            for s, n in ((kacc, FREE_ACC), (o_y, FREE_O), (d_y, FREE_DY)):
                dve.sem_inc(s, n)
            v.memset(half[:, 0:1], 1.0).then_inc(cst, 1)
            v.memset(half[:, 1:2], 0.5).then_inc(cst, 1)
            v.memset(ones[:], 1.0).then_inc(cst, 1)
            v.memset(expo[:], -0.5).then_inc(cst, 1)
            dve.wait_ge(c_exp, 1)
            v.tensor_scalar(sc_t[:, 1, :], sc_t[:, 0, :], 1.0, None, ALU.add).then_inc(c_steps, 1)
            dve.wait_ge(c_steps, 1)
            v.reciprocal(sc_t[:, 2, :], sc_t[:, 1, :]).then_inc(c_steps, 1)
            dve.wait_ge(c_steps, 2)
            v.tensor_tensor(sc[:], sc_t[:, 2, :], col[:, COL_C:COL_C + NC * B], ALU.mult).then_inc(c_steps, 1)
            dve.wait_ge(wg_hi_s, 1)
            v.tensor_tensor(wg_r[:, :, NE:2 * NE], col[:, COL_WG:COLS].rearrange("p (k e) -> p k e", k=NC),
                            wg_r[:, :, 0:NE].bitcast(f32), ALU.subtract).then_inc(c_steps, 1)
            x_stats(0)
            dve.wait_ge(mod_ps, 1)
            v.tensor_scalar(rows[:, 0, :], ps[0:B, 0, :], 1.0, None, ALU.add).then_inc(mod_sb, 1)
            x_shift(0)
            dve.wait_ge(mod_ps, 2)
            v.tensor_copy(rows[:, 1, :], ps[0:B, 1, :]).then_inc(mod_sb, 1)
            for t0 in (0, 2):
                for t in (t0, t0 + 1):
                    dve.wait_ge(bc_s, 1)
                    dve.wait_ge(xn_s, t + 1)
                    v.tensor_tensor(h1[:, t * D:(t + 1) * D], z[:, t, :], ca_bc[:], ALU.mult).then_inc(scaled0_s, 1)
                dve.wait_ge(bc_s, 2)
                for t in (t0, t0 + 1):
                    h_row(0, t)
                for t in (t0, t0 + 1):
                    h_stats(0, t)
                h_aggr(0, t0, 2)
                if t0 == 2:
                    h_shift(0, 2, 2)
                else:
                    h_shift(0, 0, 2)
            dve.wait_ge(mod_ps, 4)
            v.tensor_scalar(cb_col[:].rearrange("p (b c) -> p c b", c=NC),
                            ps[:, 0, 0:NC * B].rearrange("p (c b) -> p c b", c=NC), 1.0, None, ALU.add).then_inc(mod_sb, 1)
            for c in range(NC):
                t_split(0, c)
            dve.wait_ge(mod_ps, 5)
            guard_gates(3)
            dve.wait_ge(mod_ps, 6)
            v.tensor_copy(sb_col[:].rearrange("p (b c) -> p c b", c=NC),
                          ps[:, 1, 0:NC * B].rearrange("p (c b) -> p c b", c=NC)).then_inc(mod_sb, 1)
            dve.wait_ge(whi, 2)
            for k in range(NC):
                v.tensor_tensor(w_lo[:, WV, k, :], w_raw[1][:, k * D:(k + 1) * D],
                                w_hi[:, WV, k, :].bitcast(f32), ALU.subtract).then_inc(wlo_v, 1)
            split_lo(2)
            split_lo(3)
            dve.wait_ge(const_in, N_CONST)
            dve.wait_ge(row_out, 32)
            with dve.Fori(0, B - 1) as b:
                attention(b, False)
            attention(B - 1, True)
            split_lo(6)

            def routing(b):
                dve.wait_ge(lg_ps2, b + 1)
                v.tensor_copy(lg2[:], ps[:, SMALL_BANK, 0:NT * 2 * NE].rearrange("p (t e) -> p t e", t=NT)).then_inc(lg_s, 1)
                dve.wait_ge(lg_s, b * 2 + 1)
                v.tensor_tensor(lg[:], lg2[:, :, 0:NE], lg2[:, :, NE:2 * NE], ALU.add).then_inc(lg_s, 1)
                wait_apart(dve, lg_s, b * 2 + 2)
                for t in range(NT):
                    v.max(top8[:, t, :], lg[:, t, :]).then_inc(top_s, 1)
                dve.wait_ge(top_s, b * 5 + 4)
                v.tensor_tensor(tdif[:], top8[:, :, 0:2], top8[:, :, 0:1].to_broadcast([P, NT, 2]),
                                ALU.subtract).then_inc(top_s, 1)

            def routing_sum(b):
                dve.wait_ge(ex_s, b + 1)
                v.tensor_tensor(tsum[:], tex[:, :, 0], tex[:, :, 1], ALU.add).then_inc(lg_sum, 1)
                dve.wait_ge(lg_sum, b * 3 + 1)
                v.reciprocal(trec[:], tsum[:]).then_inc(lg_sum, 1)
                dve.wait_ge(lg_sum, b * 3 + 2)
                v.tensor_tensor(trw[:], tex[:], trec[:].rearrange("p (t o) -> p t o", o=1).to_broadcast([P, NT, 2]),
                                ALU.mult).then_inc(lg_sum, 1)
                dve.wait_ge(lg_sum, b * 3 + 3)
                v.tensor_tensor(rsum[:], trw[:, :, 0], trw[:, :, 1], ALU.add).then_inc(rsum_s, 1)

            def u_split(b, c):
                dve.wait_ge(u_his, b * NC + c + 1)
                v.scalar_tensor_tensor(g_lo[:, c, :], ps[:, U_BANKS[c % 2], :], 0.0, g_hi[:, c, :].bitcast(f32),
                                       ALU.max, ALU.subtract).then_inc(u_los, 1)

            def d_evac(b, t, last):
                n = b * NT + t
                y = tmp[:, t % 2, :]
                dve.wait_ge(d_ps, n + 1)
                dve.wait_ge(es_s, n + 1)
                if t >= 2 or last:
                    dve.wait_ge(out_s, n - 1)
                v.tensor_tensor(y, ps[:, D_BANKS[t % 2], :], es[:, t % 2, :], ALU.add).then_inc(d_y, 1)
                dve.wait_ge(d_y, n * 2 + 1 + FREE_DY)
                v.tensor_tensor(y, y, gate_bc[:, bass.ds(b * D, D)], ALU.mult).then_inc(d_y, 1)

            def ffn(b, last):
                for c in range(NC):
                    u_split(b, c)
                    if c == 0:
                        routing(b)
                    if not last:
                        x2_rows(b + B + 1, c)
                    if c == 1:
                        routing_sum(b)
                if not last:
                    h_aggr(b + B + 1, 0, NT)
                    h_shift(b + B + 1, 0, NT)
                dve.wait_ge(gb_in, B * 16)
                for c in range(NC):
                    if not last:
                        t_split(b + B + 1, c)
                    if c % 2 or last:
                        d_evac(b, c // 2 if not last else c, last)
                if not last:
                    d_evac(b, 2, last)
                    d_evac(b, 3, last)

            with dve.Fori(0, B - 1) as b:
                ffn(b, False)
            ffn(B - 1, True)

        @block.tensor
        def _(pe):
            mm = nc.tensor.matmul

            def three(dst, l_hi, l_lo, r_hi, r_lo, start, stop):
                mm(dst, l_hi, r_hi, start=start, stop=False)
                mm(dst, l_hi, r_lo, start=False, stop=False)
                return mm(dst, l_lo, r_hi, start=False, stop=stop)

            def mod_row(bank, src, sems):
                for k in range(NC):
                    pe.wait_ge(sems[k % len(sems)], 16)
                    last = mm(ps[0:B, bank, :], sc[:, k * B:(k + 1) * B], src[:, k * D:(k + 1) * D],
                              start=(k == 0), stop=(k == NC - 1))
                last.then_inc(mod_ps, 1)

            def mod_col(bank, src, s):
                pe.wait_ge(s, 16)
                for c in range(NC):
                    for k in range(NC):
                        last = mm(ps[:, bank, c * B:(c + 1) * B], src[:, k * D + c * P:k * D + (c + 1) * P],
                                  sc[:, k * B:(k + 1) * B], start=(k == 0), stop=(k == NC - 1))
                last.then_inc(mod_ps, 1)

            def transposes(g, c):
                if c == 0:
                    pe.wait_ge(z_s, g * NT + NT)
                wait(pe, t_full, g * NC + c - 1)
                for t in range(NT):
                    last = nc.tensor.transpose(ps[:, T_BANKS[c % 2], t * P:(t + 1) * P], z[:, t, c * P:(c + 1) * P], idn[:])
                last.then_inc(t_ps, 1)

            def kv_tile(b, t):
                if t == 1:
                    pe.wait_ge(o_y, (b - 1) * NT + 2 + FREE_O)
                if t >= 2:
                    pe.wait_ge(kv_sb, b * NT + t - 1)
                banks = KV_BANKS[t % 2]
                for k in range(NC):
                    if t == 0:
                        pe.wait_ge(t_los, b * NC + k + 1)
                    lo, hi = t_lo[:, k, t * P:(t + 1) * P], t_hi[:, k, t * P:(t + 1) * P]
                    for bank, r, split in zip(banks, (WK, WV), (wlo_k, wlo_v)):
                        if t == 0:
                            pe.wait_ge(split, k + 1)
                        last = three(ps[:, bank, :], hi, lo, w_hi[:, r, k, :], w_lo[:, r, k, :], k == 0, k == NC - 1)
                last.then_inc(kv_ps, 1)

            def feature_chunk(bank, r, c, s):
                for k in range(NC):
                    last = three(ps[:, bank, :], w_hi[:, r, k, c * P:(c + 1) * P], w_lo[:, r, k, c * P:(c + 1) * P],
                                 t_hi[:, k, :], t_lo[:, k, :], k == 0, k == NC - 1)
                last.then_inc(s, 1)

            def a_sums(b):
                pe.wait_ge(afold, b * 3 + 3)
                a = ps[:, SMALL_BANK, :]
                mm(a[:, 0:1], pair[:, 0, :], half[:, 1:2], start=True, stop=True)
                mm(a[:, 1:2], pair[:, 1, :], half[:, 1:2], start=True, stop=True)
                mm(a[:, 2:3], acc[:, 2 * P:3 * P], half[:, 0:1], start=True, stop=True)
                mm(a[:, 3:4], acc[:, 3 * P:4 * P], half[:, 0:1], start=True, stop=True).then_inc(a_ps, 1)

            def attention(b, last):
                for t in range(NT):
                    kv_tile(b, t)
                for c in range(NC):
                    if c == 2:
                        pe.wait_ge(kv_sb, b * NT + 3)
                    if c == 3:
                        a_sums(b)
                    if c == 0:
                        pe.wait_ge(wlo, 1)
                        pe.wait_ge(t_los, b * NC + NC)
                        pe.wait_ge(o_y, b * NT + FREE_O)
                    feature_chunk(Q_BANKS[c], WQ, c, q_ps)
                for c in range(NC):
                    pe.wait_ge(q_los, b * NC + c + 1)
                    for t in range(NT):
                        if c == 0 and t == 0:
                            pe.wait_ge(kv_sb, b * NT + NT)
                            pe.wait_ge(wlo, 2)
                        if c == 0 and t == 3:
                            pe.wait_ge(q_los, b * NC + 2)
                        done = three(ps[:, O_BANKS[t], :], g_hi[:, c, t * P:(t + 1) * P], g_lo[:, c, t * P:(t + 1) * P],
                                     w_hi[:, WO, c, :], w_lo[:, WO, c, :], c == 0, c == NC - 1)
                        if c == NC - 1:
                            done.then_inc(o_ps, 1)
                    if last:
                        if c == 0:
                            transposes(b + 1, 0)
                        if c < NC - 1:
                            transposes(b + 1, c + 1)
                    elif c == 2:
                        transposes(b + 1, 0)
                        transposes(b + 1, 1)
                    elif c == 3:
                        transposes(b + 1, 2)
                        transposes(b + 1, 3)

            pe.wait_ge(c_steps, 3)
            mod_row(0, x_slot(2), ca_w)
            mod_row(1, x_slot(3), sa_w)
            for i in range(2):
                pe.wait_ge(mod_sb, i + 1)
                mm(ps[:, 2 + i, :], ones[:], rows[0:1, i, :], start=True, stop=True).then_inc(bc_ps, 1)
            mod_row(4, x_slot(1), wm_in[2:3])
            mod_col(0, gate_bc[:], wm_in[4])
            mod_row(5, x_slot(2), wm_in[5:6])
            pe.wait_ge(ident_in, 16)
            for c in range(NC):
                transposes(0, c)
            mod_col(1, x_slot(3), wm_in[3])
            pe.wait_ge(bc_s, 2)
            pe.wait_ge(mod_sb, 9)
            with pe.Fori(0, B - 1) as b:
                attention(b, False)
            attention(B - 1, True)

            def ffn(b, last):
                pe.wait_ge(t_los, (b + B) * NC + NC)
                for k in range(NC):
                    mm(ps[0:2 * NE, SMALL_BANK, :], wg_r[:, k, :], t_hi[:, k, :], start=(k == 0), stop=False)
                    done = mm(ps[0:NE, SMALL_BANK, :], wg_r[:, k, 0:NE], t_lo[:, k, :], start=False, stop=(k == NC - 1))
                done.then_inc(lg_ps, 1)
                pe.wait_ge(wlo, 3)
                for c in range(NC):
                    if c < 2:
                        pe.wait_ge(o_y, B * NT - 1 + c + FREE_O)
                        pe.wait_ge(d_y, (b * NT + c - 2) * 2 + 1 + FREE_DY)
                    else:
                        pe.wait_ge(u_los, b * NC + c - 1)
                    feature_chunk(U_BANKS[c % 2], WUP, c, u_ps)
                    if c == 0:
                        wait_apart(pe, lg_t, b + 1)
                        for t in range(NT):
                            done = nc.tensor.transpose(ps[:, SMALL_BANK, t * 2 * NE:(t + 1) * 2 * NE],
                                                       lgt[:, t * P:(t + 1) * P], idn[0:2 * NE, 0:2 * NE])
                        done.then_inc(lg_ps2, 1)
                pe.wait_ge(wlo, 4)
                for t in range(NT):
                    for k in range(NC):
                        done = three(ps[:, E_BANKS[t], :], t_hi[:, k, t * P:(t + 1) * P], t_lo[:, k, t * P:(t + 1) * P],
                                     w_hi[:, WEXP, k, :], w_lo[:, WEXP, k, :], k == 0, k == NC - 1)
                    done.then_inc(e_ps, 1)
                if not last:
                    pe.wait_ge(lg_s, b * 2 + 1)
                    transposes(b + B + 1, 0)
                    transposes(b + B + 1, 1)
                for t in range(NT):
                    if t < 2:
                        pe.wait_ge(u_los, b * NC + NC)
                        pe.wait_ge(wlo, 5)
                    else:
                        pe.wait_ge(d_y, (b * NT + t - 2) * 2 + 1 + FREE_DY)
                    for k in range(NC):
                        done = three(ps[:, D_BANKS[t % 2], :], g_hi[:, k, t * P:(t + 1) * P], g_lo[:, k, t * P:(t + 1) * P],
                                     w_hi[:, WDOWN, k, :], w_lo[:, WDOWN, k, :], k == 0, k == NC - 1)
                    done.then_inc(d_ps, 1)
                    if t == 0 and not last:
                        transposes(b + B + 1, 2)
                        transposes(b + B + 1, 3)

            with pe.Fori(0, B - 1) as b:
                ffn(b, False)
            ffn(B - 1, True)


def layout(inputs):
    import numpy as np
    a = {k: np.asarray(v) for k, v in inputs.items()}
    half_rot = D // 4
    perm = np.concatenate([np.arange(0, 2 * half_rot, 2), np.arange(1, 2 * half_rot, 2), np.arange(2 * half_rot, D)])

    def chunks(m):
        return np.ascontiguousarray(m.reshape(NC, P, -1).transpose(1, 0, 2).reshape(P, -1))

    w_in = a["L0_attn_W_in"].reshape(D, 3, D)[:, :, perm]
    b_in = a["L0_attn_b_in"].reshape(3, D)[:, perm]
    w = [w_in[:, 1], w_in[:, 2], w_in[:, 0], a["L0_attn_W_out"][perm, :],
         a["L0_ffn_W_up"].T, a["L0_ffn_W_expert"], a["L0_ffn_W_down"].T]
    wmod = a["L0_wmod"].reshape(D, NCOMP, D)
    cols = [chunks(v.reshape(D, 1)) for v in (a["L0_attn_gamma"], a["L0_attn_beta"], b_in[0])]
    cols += [chunks(a["L0_c"].T), chunks(a["L0_ffn_W_gate"].T)]
    rot_dim = D // 2
    inv = (1.0 / 10000.0 ** (np.arange(0, rot_dim, 2, dtype=np.float32) / np.float32(rot_dim))).astype(np.float32)
    ang = (np.arange(S, dtype=np.float32)[:, None] * inv[None, :]).astype(np.float64)
    rot = np.concatenate([np.cos(2 * ang), -np.sin(2 * ang)], axis=1).astype(np.float32)
    return {
        "X": np.ascontiguousarray(a["L0_attn_X"]),
        "cols": np.ascontiguousarray(np.concatenate(cols, axis=1)),
        "ident": np.eye(P, dtype=np.float32),
        "rot": np.ascontiguousarray(rot.reshape(NT, P, -1).transpose(1, 0, 2)),
        "w": np.stack([chunks(m) for m in w]),
        "wmod": np.stack([chunks(wmod[:, i]) for i in range(NCOMP)]),
        "brow": np.ascontiguousarray(np.concatenate([b_in[1], b_in[2], a["L0_attn_b_out"]])[None, :]),
    }


def kernel(**inputs):
    import numpy as np
    import concourse.bacc as bacc
    from concourse.bass_utils import run_bass_kernel_spmd

    arrays = layout(inputs)
    nc = bacc.Bacc("TRN2", target_bir_lowering=False, num_devices=1, dynamic_dma_scratch_size=8192)
    args = {k: nc.dram_tensor(f"in_{k}", v.shape, mybir.dt.from_np(v.dtype), kind="ExternalInput").ap()
            for k, v in arrays.items()}
    out = nc.dram_tensor("out_0", (B, S, D), mybir.dt.float32, kind="ExternalOutput").ap()
    build(nc, **args, out=out)
    r = run_bass_kernel_spmd(nc, [{f"in_{k}": v for k, v in arrays.items()}], core_ids=[0])
    return r.results[0]["out_0"]
```

```python
import concourse.bass as bass
from concourse import mybir
from contextlib import ExitStack

P = 128
B, S, D = 4, 512, 512
NT = S // P
NC = D // P
ROT = D // 4
NE = 8
NCOMP = 6
EPS = 1e-5
MIN_GATE = 0.25
IDENTITY_WEIGHT = 0.5

COL_GAMMA, COL_BETA, COL_BQ, COL_C, COL_WG = 0, NC, 2 * NC, 3 * NC, 3 * NC + NC * B
COLS = COL_WG + NC * NE

WK, WV, WQ, WO = range(4)
WUP, WEXP, WDOWN = WK, WV, WQ

KV_BANKS = ((0, 1), (2, 3))
Q_BANKS = (4, 5, 0, 1)
O_BANKS = (4, 5, 2, 3)
U_BANKS = (4, 5)
E_BANKS = (0, 1, 2, 3)
D_BANKS = (4, 5)
T_BANKS = (6, 7)
SMALL_BANK = 7


def build(nc, X, cols, ident, rot, w, wmod, brow, out):
    f32 = mybir.dt.float32
    f32r = mybir.dt.float32r
    ALU = mybir.AluOpType
    ACT = mybir.ActivationFunctionType

    out_rows = out.rearrange("b (t p) d -> (b t) p d", p=P)
    x_batch = X.rearrange("b (t p) d -> b p t d", p=P)
    ROW_CA, ROW_SA, ROW_GA, ROW_GB = range(4)
    mod_rows = nc.dram_tensor("mod_rows", (4, B, D), f32, kind="Internal").ap()

    ctx = ExitStack()
    with ctx:
        def sb(name, shape, dt=f32):
            return ctx.enter_context(nc.sbuf_tensor(name, shape, dt))

        def sem(name):
            return ctx.enter_context(nc.semaphore(name))

        w_hi = sb("w_hi", [P, 4, NC, D], f32r)
        w_lo = sb("w_lo", [P, 4, NC, D], f32r)
        wg_r = sb("wg_r", [P, NC, 2 * NE], f32r)
        stage = sb("stage", [P, 2, NC * D])
        t_hi = sb("t_hi", [P, NC, S], f32r)
        t_lo = sb("t_lo", [P, NC, S], f32r)
        g_hi = sb("g_hi", [P, NC, S], f32r)
        g_lo = sb("g_lo", [P, NC, S], f32r)
        xs = sb("xs", [P, B * NT * D])
        h1 = sb("h1", [P, NT * D])
        z = sb("z", [P, NT, D])
        ca_bc = sb("ca_bc", [P, D])
        sa_bc = sb("sa_bc", [P, D])
        gate_bc = sb("gate_bc", [P, B * D])
        bkv_bc = sb("bkv_bc", [P, 2, D])
        bo_bc = sb("bo_bc", [P, D])
        rot_sb = sb("rot_sb", [P, NT, 2 * ROT])
        kv = sb("kv", [P, 2, 2, D])
        prod = sb("prod", [P, D + 2 * ROT])
        cross = sb("cross", [P, 2 * ROT])
        acc = sb("acc", [P, D + 2 * ROT])
        full = sb("full", [P, 2, S])
        tmp = sb("tmp", [P, NT, D])
        es = kv[:, :, 0, :]
        rows = kv[0:B, :, 0, :]
        gate_rows = tmp[0:B, 0:2]
        sign = kv[0:B, :, 1, :]
        gate_abs = tmp[0:B, 2:4]
        col = sb("col", [P, COLS])
        idn = sb("idn", [P, P])
        half = sb("half", [P, 2])
        ones = sb("ones", [1, P])
        expo = sb("expo", [P, NT])
        sc = sb("sc", [P, NC * B])
        sc_t = sb("sc_t", [P, 3, NC * B])
        cb_col = sb("cb_col", [P, B * NC])
        sb_col = sb("sb_col", [P, B * NC])
        xsum = sb("xsum", [P, NT])
        xmn = sb("xmn", [P, NT])
        xss = sb("xss", [P, NT])
        xst = sb("xst", [P, NT, 6])
        xmv = sb("xmv", [P, NT, 2])
        xve = sb("xve", [P, NT])
        xrs = sb("xrs", [P, NT])
        xnm = sb("xnm", [P, NT])
        hst = sb("hst", [P, NT, 6])
        hmv = sb("hmv", [P, NT, 2])
        hve = sb("hve", [P, NT])
        hrs = sb("hrs", [P, NT])
        hnm = sb("hnm", [P, NT])
        nsq = sb("nsq", [P, 2, 2])
        rnm = sb("rnm", [P, 2, 2])
        wgt = sb("wgt", [P, 2])
        fold = sb("fold", [P, 2, ROT])
        pair = sb("pair", [P, 2, ROT])
        sqj = sb("sqj", [P, D], mybir.dt.bfloat16)
        xjunk = sb("xjunk", [P, D], mybir.dt.bfloat16)
        a_col = sb("a_col", [P, NC])
        ab_col = sb("ab_col", [P, NC])
        lgt = sb("lgt", [2 * NE, S])
        lg2 = sb("lg2", [P, NT, 2 * NE])
        lg = sb("lg", [P, NT, NE])
        top8 = sb("top8", [P, NT, 8])
        tdif = sb("tdif", [P, NT, 2])
        tex = sb("tex", [P, NT, 2])
        tsum = sb("tsum", [P, NT])
        trec = sb("trec", [P, NT])
        trw = sb("trw", [P, NT, 2])
        rsum = sb("rsum", [P, NT])
        ps = ctx.enter_context(nc.psum_tensor("ps", [P, 8, 512], f32))

        col_in = sem("col_in")
        const_in = sem("const_in")
        ident_in = sem("ident_in")
        x_in = sem("x_in")
        wm_in = [sem(f"wm_in{i}") for i in range(NCOMP)]
        ca_w = [sem(f"ca_w{k}") for k in range(NC)]
        sa_w = [sem(f"sa_w{k}") for k in range(NC)]
        wkv_in = [[sem(f"wkv_in{k}{i}") for i in range(2)] for k in range(NC)]
        w_in = [sem(f"w_in{i}") for i in range(7)]
        ca_in = sem("ca_in")
        ga_in = sem("ga_in")
        gb_in = sem("gb_in")
        row_out = sem("row_out")
        gate_out = sem("gate_out")
        out_dma = sem("out_dma")
        waits_done = sem("waits_done")
        cst = sem("cst")
        c_exp = sem("c_exp")
        c_steps = sem("c_steps")
        wg_hi_s = sem("wg_hi_s")
        mod_ps = sem("mod_ps")
        mod_sb = sem("mod_sb")
        gate_abs_s = sem("gate_abs_s")
        bc_ps = sem("bc_ps")
        whi_k, whi_v = sem("whi_k"), sem("whi_v")
        whi = sem("whi")
        wlo = sem("wlo")
        wlo_k, wlo_v = sem("wlo_k"), sem("wlo_v")
        wlo_out = sem("wlo_out")
        wlo_expert, wlo_down = sem("wlo_expert"), sem("wlo_down")
        xst_s, xmv_s = sem("xst_s"), sem("xmv_s")
        xsum_s = sem("xsum_s")
        xmn_s = sem("xmn_s")
        xve_s = sem("xve_s")
        xrs_s = sem("xrs_s")
        xnm_s = sem("xnm_s")
        xn_s = sem("xn_s")
        scaled0_s = sem("scaled0_s")
        scaled_s = sem("scaled_s")
        h1_s = sem("h1_s")
        base_s = sem("base_s")
        hst_s, hmv_s = sem("hst_s"), sem("hmv_s")
        hve_s = sem("hve_s")
        hrs_s = sem("hrs_s")
        hnm_s = sem("hnm_s")
        z_s = sem("z_s")
        t_ps, t_full, t_his, t_los = sem("t_ps"), sem("t_full"), sem("t_his"), sem("t_los")
        kv_ps, kv_sb = sem("kv_ps"), sem("kv_sb")
        nsq_s = sem("nsq_s")
        rnm_s = sem("rnm_s")
        wgt_s = sem("wgt_s")
        kprod, kcross = sem("kprod"), sem("kcross")
        krot = sem("krot")
        kacc = sem("kacc")
        afold = sem("afold")
        a_ps, a_sb = sem("a_ps"), sem("a_sb")
        ab_sb = sem("ab_sb")
        q_ps, q_full, q_his, q_los = sem("q_ps"), sem("q_full"), sem("q_his"), sem("q_los")
        o_ps, o_y = sem("o_ps"), sem("o_y")
        og_dve, x2_dve = sem("og_dve"), sem("x2_dve")
        og_pool, x2_pool = sem("og_pool"), sem("x2_pool")
        lg_ps, lg_t = sem("lg_ps"), sem("lg_t")
        lg_ps2 = sem("lg_ps2")
        lg_s = sem("lg_s")
        top_s = sem("top_s")
        ex_s = sem("ex_s")
        lg_sum, rsum_s = sem("lg_sum"), sem("rsum_s")
        u_ps, u_his, u_los = sem("u_ps"), sem("u_his"), sem("u_los")
        e_ps, es_s = sem("e_ps"), sem("es_s")
        d_ps = sem("d_ps")
        d_y = sem("d_y")
        out_s = sem("out_s")
        eg_s = sem("eg_s")
        last_out = sem("last_out")

        block = ctx.enter_context(nc.Block())

        FREE_NSQ, FREE_RNM, FREE_ACC, FREE_O, FREE_DY = 4, 2, 1, NT, 4


        def is_first(b):
            return isinstance(b, int) and b == 0

        def wait(eng, s, v):
            if not (isinstance(v, int) and v <= 0):
                eng.wait_ge(s, v)

        def tok(b, t):
            return bass.ds((b * NT + t) * D, D)

        def x_slot(b):
            return xs[:, b * NT * D:(b + 1) * NT * D]

        def wait_apart(eng, s, v):
            eng.wait_ge(s, v)
            eng.sem_inc(waits_done, 1)

        N_CONST = 3 * 16
        ALL, LEFT, RIGHT = slice(0, D), slice(0, D // 2), slice(D // 2, D)
        LAST_PARTS = [(0, ALL, 4), (1, ALL, 5), (2, ALL, 6), (3, LEFT, 7), (3, RIGHT, 4)]
        W_ORDER = (WK, WV, WQ, WO, WUP, WEXP, WDOWN)
        w_raw = (stage[:, 0, :], stage[:, 1, :], x_slot(2), stage[:, 0, :], stage[:, 1, :], stage[:, 0, :], stage[:, 1, :])

        @block.sync
        def _(sp):
            sp.dma_start(col[:], cols).then_inc(col_in, 16)
            for k in range(NC):
                sp.dma_start(x_slot(2)[:, k * D:(k + 1) * D], wmod[1][:, k * D:(k + 1) * D]).then_inc(ca_w[k], 16)
            sp.dma_start(x_slot(0).rearrange("p (t d) -> p t d", t=NT), x_batch[0]).then_inc(x_in, 16)
            for k in range(NC):
                sp.dma_start(x_slot(3)[:, k * D:(k + 1) * D], wmod[0][:, k * D:(k + 1) * D]).then_inc(sa_w[k], 16)
            sp.dma_start(x_slot(1), wmod[2]).then_inc(wm_in[2], 16)
            sp.dma_start(gate_bc[:], wmod[4]).then_inc(wm_in[4], 16)
            sp.dma_start(idn[:], ident).then_inc(ident_in, 16)
            sp.wait_ge(mod_ps, 1)
            sp.dma_start(x_slot(2), wmod[5]).then_inc(wm_in[5], 16)
            sp.wait_ge(mod_ps, 2)
            sp.dma_start(x_slot(3), wmod[3]).then_inc(wm_in[3], 16)
            for k in range(NC):
                for i in range(2):
                    sp.dma_start(w_raw[i][:, k * D:(k + 1) * D], w[i][:, k * D:(k + 1) * D]).then_inc(wkv_in[k][i], 16)
            sp.wait_ge(mod_ps, 5)
            sp.dma_start(w_raw[2], w[2]).then_inc(w_in[2], 16)
            sp.wait_ge(mod_sb, 2)
            sp.dma_start(mod_rows[ROW_CA], rows[:, 0, :]).then_inc(row_out, 16)
            sp.dma_start(mod_rows[ROW_SA], rows[:, 1, :]).then_inc(row_out, 16)
            sp.wait_ge(mod_sb, 5)
            sp.dma_start(mod_rows[ROW_GA], gate_rows[:, 0, :]).then_inc(gate_out, 16)
            sp.dma_start(mod_rows[ROW_GB], gate_rows[:, 1, :]).then_inc(gate_out, 16)
            sp.dma_start(bkv_bc[:].rearrange("p a d -> p (a d)"), brow[0:1, 0:2 * D].to_broadcast([P, 2 * D])).then_inc(const_in, 16)
            sp.dma_start(rot_sb[:], rot).then_inc(const_in, 16)
            sp.dma_start(bo_bc[:], brow[0:1, 2 * D:3 * D].to_broadcast([P, D])).then_inc(const_in, 16)

            def load_x(b):
                sp.wait_ge(x_in, b * 16)
                sp.dma_start(x_slot(b).rearrange("p (t d) -> p t d", t=NT), x_batch[b]).then_inc(x_in, 16)

            def load_modulation(b):
                sp.wait_ge(h1_s, b * NT)
                sp.dma_start(ca_bc[:], mod_rows[ROW_CA, bass.ds(b, 1), :].to_broadcast([P, D])).then_inc(ca_in, 16)
                sp.dma_start(sa_bc[:], mod_rows[ROW_SA, bass.ds(b, 1), :].to_broadcast([P, D])).then_inc(ca_in, 16)

            sp.wait_ge(gate_out, 32)
            for b in range(B):
                sp.dma_start(gate_bc[:, b * D:(b + 1) * D],
                             mod_rows[ROW_GA, b:b + 1, :].to_broadcast([P, D])).then_inc(ga_in, 16)
            load_x(1)
            sp.wait_ge(wlo_k, NC)
            sp.dma_start(w_raw[3], w[3]).then_inc(w_in[3], 16)
            sp.wait_ge(row_out, 32)
            load_modulation(1)
            sp.wait_ge(wlo, 1)
            load_x(2)
            sp.wait_ge(mod_ps, 6)
            load_x(3)
            sp.wait_ge(wlo_v, NC)
            sp.dma_start(w_raw[4], w[4]).then_inc(w_in[4], 16)
            with sp.Fori(2, B) as b:
                load_modulation(b)
            sp.wait_ge(wlo_out, NC)
            sp.dma_start(w_raw[5], w[5]).then_inc(w_in[5], 16)
            sp.wait_ge(wlo, 2)
            sp.dma_start(w_raw[6], w[6]).then_inc(w_in[6], 16)
            sp.wait_ge(x2_dve, B * 2)
            sp.wait_ge(x2_pool, B * 2)
            for b in range(B):
                sp.dma_start(gate_bc[:, b * D:(b + 1) * D],
                             mod_rows[ROW_GB, b:b + 1, :].to_broadcast([P, D])).then_inc(gb_in, 16)
            with sp.Fori(0, (B - 1) * NT) as i:
                sp.wait_ge(out_s, i + 1)
                sp.dma_start(out_rows[bass.ds(i, 1)].rearrange("o p d -> (o p) d"),
                             xs[:, bass.ds(i * D, D)]).then_inc(out_dma, 16)
            for i, (t, part, _) in enumerate(LAST_PARTS):
                sp.wait_ge(last_out, i + 1)
                sp.dma_start(out_rows[(B - 1) * NT + t][:, part], xs[:, tok(B - 1, t)][:, part]).then_inc(out_dma, 16)
            sp.wait_ge(out_dma, ((B - 1) * NT + len(LAST_PARTS)) * 16)

        @block.gpsimd
        def _(pool):
            def power(dst, src, n, s, steps=1):
                nc.gpsimd.tensor_tensor(dst, src, expo[:, 0:n], ALU.pow).then_inc(s, steps)

            def rstd_x(g):
                pool.wait_ge(xve_s, g + 1)
                power(xrs[:], xve[:], NT, xrs_s)

            def rstd_h(g, t0, n):
                pool.wait_ge(hve_s, g * NT + t0 + n)
                wait(pool, z_s, g * NT)
                power(hrs[:, t0:t0 + n], hve[:, t0:t0 + n], n, hrs_s, n)

            def low_part(i, hi_ready, counts, s):
                for k in range(NC):
                    pool.wait_ge(hi_ready, counts[k])
                    nc.gpsimd.tensor_tensor(w_lo[:, W_ORDER[i], k, :], w_raw[i][:, k * D:(k + 1) * D],
                                            w_hi[:, W_ORDER[i], k, :].bitcast(f32), ALU.subtract).then_inc(s, 1)

            def weight(b, t):
                pool.wait_ge(nsq_s, (b * NT + t) * 2 + 2 + FREE_NSQ)
                power(rnm[:, t % 2, :], nsq[:, t % 2, :], 2, rnm_s)
                pool.wait_ge(rnm_s, b * NT + t + 1 + FREE_RNM)
                nc.gpsimd.tensor_tensor(wgt[:, t % 2:t % 2 + 1], rnm[:, t % 2, 0:1], rnm[:, t % 2, 1:2],
                                        ALU.mult).then_inc(wgt_s, 1)

            def x2_out(b, t):
                wait_apart(pool, o_y, b * NT + NT + FREE_O)
                nc.gpsimd.tensor_tensor(tmp[:, t, :], tmp[:, t, :], gate_bc[:, bass.ds(b * D, D)], ALU.mult).then_inc(og_pool, 1)
                wait_apart(pool, og_pool, b * 2 + t - 1)
                nc.gpsimd.tensor_tensor(xs[:, tok(b, t)], xs[:, tok(b, t)], tmp[:, t, :], ALU.add).then_inc(x2_pool, 1)

            def base(g, t):
                pool.wait_ge(z_s, g * NT + t + 1)
                if not is_first(g):
                    pool.wait_ge(x2_dve if t < 2 else x2_pool, (g - 1) * 2 + t % 2 + 1)
                nc.gpsimd.tensor_tensor(tmp[:, t, :], h1[:, t * D:(t + 1) * D], bo_bc[:], ALU.add).then_inc(base_s, 1)

            def scale_rows(g, t):
                pool.wait_ge(xn_s, g * NT + t + 1)
                pool.wait_ge(base_s, (g - 1) * NT + t + 1)
                if t == 0:
                    pool.wait_ge(ca_in, g * 32)
                nc.gpsimd.tensor_tensor(h1[:, t * D:(t + 1) * D], z[:, t, :], ca_bc[:], ALU.mult).then_inc(scaled_s, 1)

            def attention(b, last):
                if not is_first(b):
                    x2_out(b - 1, 2)
                weight(b, 0)
                if not is_first(b):
                    x2_out(b - 1, 3)
                weight(b, 1)
                base(b, 0)
                base(b, 1)
                weight(b, 2)
                if not last:
                    rstd_x(b + 1)
                base(b, 2)
                weight(b, 3)
                if not last:
                    scale_rows(b + 1, 0)
                    scale_rows(b + 1, 1)
                base(b, 3)
                if not last:
                    scale_rows(b + 1, 2)
                    scale_rows(b + 1, 3)
                    rstd_h(b + 1, 0, 2)
                    rstd_h(b + 1, 2, 2)
                else:
                    rstd_h(b + 1, 0, NT)
                    low_part(5, whi, (4,) * NC, wlo_expert)

            pool.sem_inc(rnm_s, FREE_RNM)
            pool.wait_ge(cst, 4)
            rstd_x(0)
            rstd_h(0, 0, 2)
            rstd_h(0, 2, 2)
            low_part(0, whi_k, (1, 2, 3, 4), wlo_k)
            pool.wait_ge(gate_out, 32)
            pool.wait_ge(const_in, N_CONST)
            attention(0, False)
            pool.wait_ge(ga_in, B * 16)
            with pool.Fori(1, B - 1) as b:
                attention(b, False)
            attention(B - 1, True)
            x2_out(B - 1, 2)
            x2_out(B - 1, 3)
            low_part(6, whi, (5,) * NC, wlo_down)
            with pool.Fori(0, B - 1) as b:
                rstd_h(b + B + 1, 0, NT)

        @block.scalar
        def _(act):
            def split_hi(i):
                act.wait_ge(w_in[i], 16)
                if i == 4:
                    act.wait_ge(kv_ps, B * NT)
                if i == 6:
                    act.wait_ge(q_ps, B * NC)
                nc.scalar.activation(w_hi[:, W_ORDER[i]].rearrange("p k n -> p (k n)"), w_raw[i], ACT.Copy).then_inc(whi, 1)

            def norm_sums(b, t):
                act.wait_ge(kv_sb, b * NT + t + 1)
                act.wait_ge(rnm_s, b * NT + t - 1 + FREE_RNM)
                for i in range(2):
                    act.wait_ge(nsq_s, (b * NT + t) * 2 + i + FREE_NSQ)
                    nc.scalar.activation(sqj[:], kv[:, t % 2, i, :], ACT.Square,
                                         accum_out=nsq[:, t % 2, i:i + 1]).then_inc(nsq_s, 1)

            def split_hi_k(k):
                act.wait_ge(wkv_in[k][0], 16)
                nc.scalar.activation(w_hi[:, WK, k, :], w_raw[0][:, k * D:(k + 1) * D], ACT.Copy).then_inc(whi_k, 1)

            def x_sums(g):
                act.wait_ge(x_in, g * 16 + 16)
                for t in range(NT):
                    if not (isinstance(g, int) and t == 0):
                        wait_apart(act, xsum_s, (g - 1) * 2 * NT + t)
                    nc.scalar.activation(xjunk[:], xs[:, tok(g, t)], ACT.Identity,
                                         accum_out=xsum[:, t:t + 1]).then_inc(xsum_s, 1)

            def x_squares(g):
                act.wait_ge(xmn_s, g)
                for t in range(NT):
                    wait_apart(act, xsum_s, (g - 1) * 2 * NT + NT + t)
                    nc.scalar.activation(xjunk[:], xs[:, tok(g, t)], ACT.Square, bias=xmn[:, t:t + 1],
                                         accum_out=xss[:, t:t + 1]).then_inc(xsum_s, 1)

            def normalise_x(g, t0, n):
                wait(act, t_ps, g * NC)
                wait_apart(act, xnm_s, g + 1)
                for t in range(t0, t0 + n):
                    nc.scalar.activation(z[:, t, :], xs[:, tok(g, t)], ACT.Identity, bias=xnm[:, t:t + 1],
                                         scale=xrs[:, t:t + 1]).then_inc(xn_s, 1)

            def normalise(g, t0, n, ffn):
                act.wait_ge(hnm_s, g * NT + t0 + n)
                if t0 == 0:
                    wait(act, t_ps, g * NC)
                for t in range(t0, t0 + n):
                    src = xs[:, tok(g - B, t)] if ffn else h1[:, t * D:(t + 1) * D]
                    nc.scalar.activation(z[:, t, :], src, ACT.Identity, bias=hnm[:, t:t + 1],
                                         scale=hrs[:, t:t + 1]).then_inc(z_s, 1)

            def t_evac(g, c, ffn, after_q=False):
                n = g * NC + c
                act.wait_ge(t_ps, n + 1)
                if after_q and c < 2:
                    act.wait_ge(q_los, n - 1)
                else:
                    wait(act, t_los, n - 1)
                if ffn:
                    j = bass.ds((g - B) * NC + c, 1)
                    scale, bias = cb_col[:, j], sb_col[:, j]
                else:
                    scale, bias = col[:, COL_GAMMA + c:COL_GAMMA + c + 1], col[:, COL_BETA + c:COL_BETA + c + 1]
                nc.scalar.activation(full[:, c % 2, :], ps[:, T_BANKS[c % 2], :], ACT.Identity,
                                     bias=bias, scale=scale).then_inc(t_full, 1)
                act.wait_ge(t_full, n + 1)
                nc.scalar.activation(t_hi[:, c, :], full[:, c % 2, :], ACT.Copy).then_inc(t_his, 1)

            def q_evac(b, c):
                n = b * NC + c
                act.wait_ge(q_ps, n + 1)
                if c == 0:
                    act.wait_ge(ab_sb, b + 1)
                if c >= 2:
                    act.wait_ge(q_los, n - 1)
                else:
                    act.wait_ge(t_los, n + 3)
                nc.scalar.activation(full[:, c % 2, :], ps[:, Q_BANKS[c], :], ACT.Identity,
                                     bias=ab_col[:, c:c + 1], scale=a_col[:, c:c + 1]).then_inc(q_full, 1)
                act.wait_ge(q_full, n + 1)
                nc.scalar.activation(g_hi[:, c, :], full[:, c % 2, :], ACT.Copy).then_inc(q_his, 1)

            def u_evac(b, c):
                act.wait_ge(u_ps, b * NC + c + 1)
                nc.scalar.activation(g_hi[:, c, :], ps[:, U_BANKS[c % 2], :], ACT.Relu).then_inc(u_his, 1)

            def e_evac(b, t, last):
                act.wait_ge(e_ps, b * NT + t + 1)
                if t == 0:
                    act.wait_ge(rsum_s, b + 1)
                if last and t >= 2:
                    act.wait_ge(eg_s, 2 * (t - 2) + 2)
                else:
                    act.wait_ge(d_y, (b * NT + t - 2) * 2 + 1 + FREE_DY)
                nc.scalar.activation(es[:, t % 2, :], ps[:, E_BANKS[t], :], ACT.Copy,
                                     scale=rsum[:, t:t + 1]).then_inc(es_s, 1)

            def attention(b, last):
                for t in range(NT):
                    if is_first(b) and t == 2:
                        split_hi(3)
                    norm_sums(b, t)
                    if t == 0 and not last:
                        x_sums(b + 1)
                    if t == 1 and not last:
                        x_squares(b + 1)
                if not last:
                    normalise_x(b + 1, 0, NT)
                if last:
                    split_hi(4)
                    split_hi(5)
                for c in range(NC):
                    if c == 2 and last:
                        normalise(b + 1, 0, NT, True)
                    q_evac(b, c)
                if not last:
                    normalise(b + 1, 0, 2, False)
                    normalise(b + 1, 2, 2, False)
                for c in range(NC):
                    if c == 0:
                        act.wait_ge(q_ps, b * NC + NC)
                    t_evac(b + 1, c, last, after_q=True)

            act.sem_inc(nsq_s, FREE_NSQ)
            act.wait_ge(col_in, 16)
            nc.scalar.activation(sc_t[:, 0, :], col[:, COL_C:COL_C + NC * B], ACT.Exp, scale=-1.0).then_inc(c_exp, 1)
            nc.scalar.activation(wg_r[:, :, 0:NE], col[:, COL_WG:COLS].rearrange("p (k e) -> p k e", k=NC),
                                 ACT.Copy).then_inc(wg_hi_s, 1)
            normalise_x(0, 0, NT)
            normalise(0, 0, 2, False)
            normalise(0, 2, 2, False)
            act.wait_ge(mod_ps, 5)
            nc.scalar.activation(gate_abs, ps[0:B, 4:6, :], ACT.Abs, scale=2.0).then_inc(gate_abs_s, 1)
            for c in range(NC):
                split_hi_k(c)
                t_evac(0, c, False)
            split_hi(2)
            act.wait_ge(mod_sb, 6)
            attention(0, False)
            with act.Fori(1, B - 1) as b:
                attention(b, False)
            attention(B - 1, True)
            split_hi(6)

            def ffn(b, last):
                act.wait_ge(lg_ps, b + 1)
                nc.scalar.activation(lgt[:], ps[0:2 * NE, SMALL_BANK, :], ACT.Copy).then_inc(lg_t, 1)
                for c in range(NC):
                    u_evac(b, c)
                    if c == 1:
                        act.wait_ge(top_s, b * 5 + 5)
                        nc.scalar.activation(tex[:], tdif[:], ACT.Exp).then_inc(ex_s, 1)
                if not last:
                    normalise(b + B + 1, 0, NT, True)
                for c in range(NC):
                    if not last:
                        if c == 0:
                            act.wait_ge(e_ps, b * NT + NT)
                        t_evac(b + B + 1, c, True)
                    if c % 2 or last:
                        e_evac(b, c // 2 if not last else c, last)
                if not last:
                    e_evac(b, 2, last)
                    e_evac(b, 3, last)

            with act.Fori(0, B - 1) as b:
                ffn(b, False)
            ffn(B - 1, True)

        @block.vector
        def _(dve):
            v = nc.vector

            def split_lo(i):
                dve.wait_ge(whi, i - 1)
                if i == 4:
                    dve.wait_ge(kv_ps, B * NT)
                r = W_ORDER[i]
                v.tensor_tensor(w_lo[:, r].rearrange("p k n -> p (k n)"), w_raw[i],
                                w_hi[:, r].rearrange("p k n -> p (k n)").bitcast(f32), ALU.subtract).then_inc(wlo, 1)

            def split_lo_out(k):
                dve.wait_ge(whi, 2)
                v.tensor_tensor(w_lo[:, WO, k, :], w_raw[3][:, k * D:(k + 1) * D],
                                w_hi[:, WO, k, :].bitcast(f32), ALU.subtract).then_inc(wlo_out, 1)

            def x_stats(g, t0, n):
                if t0 == 0:
                    dve.wait_ge(x_in, g * 16 + 16)
                for t in range(t0, t0 + n):
                    v.bn_stats(xst[:, t, :], xs[:, tok(g, t)]).then_inc(xst_s, 1)

            def x_aggr(g):
                for t in range(NT):
                    wait_apart(dve, xst_s, g * NT + t + 1)
                    v.bn_aggr(xmv[:, t, :], xst[:, t, :]).then_inc(xmv_s, 1)
                dve.wait_ge(xmv_s, g * NT + NT)
                v.tensor_scalar(xve[:], xmv[:, :, 1], EPS, None, ALU.add).then_inc(xve_s, 1)

            def x_mean(g):
                dve.wait_ge(xsum_s, (g - 1) * 2 * NT + NT)
                v.tensor_scalar(xmn[:], xsum[:], -1.0 / D, None, ALU.mult).then_inc(xmn_s, 1)

            def x_var(g):
                dve.wait_ge(xsum_s, g * 2 * NT)
                v.tensor_scalar(xve[:], xss[:], 1.0 / D, EPS, ALU.mult, ALU.add).then_inc(xve_s, 1)

            def x_shift(g):
                dve.wait_ge(xrs_s, g + 1)
                if is_first(g):
                    v.scalar_tensor_tensor(xnm[:], xmv[:, :, 0], -1.0, xrs[:], ALU.mult, ALU.mult).then_inc(xnm_s, 1)
                else:
                    dve.wait_ge(xmn_s, g)
                    v.tensor_tensor(xnm[:], xmn[:], xrs[:], ALU.mult).then_inc(xnm_s, 1)

            def h_row(g, t):
                n = g * NT + t
                h = h1[:, t * D:(t + 1) * D]
                if is_first(g):
                    dve.wait_ge(scaled0_s, t + 1)
                    v.tensor_tensor(h, h, ps[:, 3, :], ALU.add).then_inc(h1_s, 1)
                else:
                    dve.wait_ge(scaled_s, n + 1 - NT)
                    v.tensor_tensor(h, h, sa_bc[:], ALU.add).then_inc(h1_s, 1)

            def h_stats(g, t):
                dve.wait_ge(h1_s, g * NT + t + 1)
                v.bn_stats(hst[:, t, :], h1[:, t * D:(t + 1) * D]).then_inc(hst_s, 1)

            def x2_rows(g, t):
                if t == 0:
                    wait_apart(dve, x2_dve, (g - B + 1) * 2)
                    wait_apart(dve, x2_pool, (g - B + 1) * 2)
                v.bn_stats(hst[:, t, :], xs[:, tok(g - B, t)]).then_inc(hst_s, 1)

            def h_aggr(g, t0, n):
                for t in range(t0, t0 + n):
                    wait_apart(dve, hst_s, g * NT + t + 1)
                    v.bn_aggr(hmv[:, t, :], hst[:, t, :]).then_inc(hmv_s, 1)
                dve.wait_ge(hmv_s, g * NT + t0 + n)
                v.tensor_scalar(hve[:, t0:t0 + n], hmv[:, t0:t0 + n, 1], EPS, None, ALU.add).then_inc(hve_s, n)

            def h_shift(g, t0, n):
                dve.wait_ge(hrs_s, g * NT + t0 + n)
                v.scalar_tensor_tensor(hnm[:, t0:t0 + n], hmv[:, t0:t0 + n, 0], -1.0, hrs[:, t0:t0 + n],
                                       ALU.mult, ALU.mult).then_inc(hnm_s, n)

            def t_split(g, c):
                dve.wait_ge(t_his, g * NC + c + 1)
                v.tensor_tensor(t_lo[:, c, :], full[:, c % 2, :], t_hi[:, c, :].bitcast(f32),
                                ALU.subtract).then_inc(t_los, 1)

            def kv_rows(b, t):
                n = b * NT + t
                banks = KV_BANKS[t % 2]
                dve.wait_ge(kv_ps, n + 1)
                dve.wait_ge(nsq_s, (n - 1) * 2 + FREE_NSQ)
                v.tensor_tensor(kv[:, t % 2], ps[:, banks[0]:banks[0] + 2, :], bkv_bc[:], ALU.add).then_inc(kv_sb, 1)

            def kv_products(b, t):
                n = b * NT + t
                k, val = kv[:, t % 2, 0, :], kv[:, t % 2, 1, :]
                dve.wait_ge(kv_sb, n + 1)
                v.tensor_tensor(cross[:, 0:ROT], k[:, 0:ROT], val[:, ROT:2 * ROT], ALU.mult).then_inc(kcross, 1)
                v.tensor_tensor(cross[:, ROT:2 * ROT], k[:, ROT:2 * ROT], val[:, 0:ROT], ALU.mult).then_inc(kcross, 1)
                dve.wait_ge(kacc, n + FREE_ACC)
                v.tensor_tensor(prod[:, 0:D], k, val, ALU.mult).then_inc(kprod, 1)
                dve.wait_ge(kcross, n * 2 + 2)
                v.tensor_tensor(prod[:, D + ROT:D + 2 * ROT], cross[:, 0:ROT], cross[:, ROT:2 * ROT],
                                ALU.add).then_inc(krot, 1)
                dve.wait_ge(kprod, n + 1)
                v.tensor_tensor(prod[:, D:D + ROT], prod[:, 0:ROT], prod[:, ROT:2 * ROT], ALU.subtract).then_inc(krot, 1)
                dve.wait_ge(krot, n * 3 + 2)
                v.tensor_tensor(prod[:, D:D + 2 * ROT], prod[:, D:D + 2 * ROT], rot_sb[:, t, :],
                                ALU.mult).then_inc(krot, 1)

            def kv_sum(b, t):
                n = b * NT + t
                dve.wait_ge(krot, n * 3 + 3)
                dve.wait_ge(wgt_s, n + 1)
                if t == 0:
                    v.tensor_scalar(acc[:], prod[:], wgt[:, 0:1], None, ALU.mult).then_inc(kacc, 1)
                else:
                    dve.wait_ge(kacc, n + FREE_ACC)
                    v.scalar_tensor_tensor(acc[:], prod[:], wgt[:, t % 2:t % 2 + 1], acc[:],
                                           ALU.mult, ALU.add).then_inc(kacc, 1)

            def a_pairs(b):
                dve.wait_ge(kacc, b * NT + NT + FREE_ACC)
                blocks = acc[:].rearrange("p (g i r) -> p g i r", g=3, i=2)
                v.tensor_tensor(fold[:], blocks[:, 0:3:2, 0, :], blocks[:, 0:3:2, 1, :], ALU.add).then_inc(afold, 1)
                dve.wait_ge(afold, b * 3 + 1)
                v.tensor_tensor(pair[:, 0, :], fold[:, 0, :], fold[:, 1, :], ALU.add).then_inc(afold, 1)
                v.tensor_tensor(pair[:, 1, :], fold[:, 0, :], fold[:, 1, :], ALU.subtract).then_inc(afold, 1)

            def a_evac(b):
                dve.wait_ge(a_ps, b + 1)
                v.tensor_scalar(a_col[:], ps[:, SMALL_BANK, 0:NC], 1.0 - IDENTITY_WEIGHT, IDENTITY_WEIGHT,
                                ALU.mult, ALU.add).then_inc(a_sb, 1)
                dve.wait_ge(a_sb, b + 1)
                v.tensor_tensor(ab_col[:], a_col[:], col[:, COL_BQ:COL_BQ + NC], ALU.mult).then_inc(ab_sb, 1)

            def q_split(b, c):
                dve.wait_ge(q_his, b * NC + c + 1)
                v.tensor_tensor(g_lo[:, c, :], full[:, c % 2, :], g_hi[:, c, :].bitcast(f32),
                                ALU.subtract).then_inc(q_los, 1)

            def o_evac(b, t):
                n = b * NT + t
                dve.wait_ge(o_ps, n + 1)
                dve.wait_ge(base_s, n + 1)
                v.tensor_tensor(tmp[:, t, :], ps[:, O_BANKS[t], :], tmp[:, t, :], ALU.add).then_inc(o_y, 1)

            def x2_out(b, t):
                dve.wait_ge(o_y, b * NT + NT + FREE_O)
                v.tensor_tensor(tmp[:, t, :], tmp[:, t, :], gate_bc[:, bass.ds(b * D, D)], ALU.mult).then_inc(og_dve, 1)
                dve.wait_ge(og_dve, b * 2 + t + 1)
                v.tensor_tensor(xs[:, tok(b, t)], xs[:, tok(b, t)], tmp[:, t, :], ALU.add).then_inc(x2_dve, 1)

            def attention(b, last):
                for t in range(NT):
                    kv_rows(b, t)
                    if t > 0:
                        kv_sum(b, t - 1)
                    if not last and t == 1:
                        x_mean(b + 1)
                    if not last and t == 2:
                        x_var(b + 1)
                    if not last and t == 3:
                        x_shift(b + 1)
                    kv_products(b, t)
                    if t < 2 and not is_first(b):
                        x2_out(b - 1, t)
                    if is_first(b) and t == 2:
                        split_lo_out(0)
                        split_lo_out(1)
                kv_sum(b, NT - 1)
                a_pairs(b)
                if last:
                    x2_rows(B, 0)
                    x2_rows(B, 1)
                    a_evac(b)
                    x2_rows(B, 2)
                    x2_rows(B, 3)
                    h_aggr(B, 0, NT)
                    q_split(b, 0)
                    q_split(b, 1)
                    h_shift(B, 0, NT)
                    split_lo(4)
                    q_split(b, 2)
                    q_split(b, 3)
                else:
                    dve.wait_ge(ca_in, b * 32 + 32)
                    h_row(b + 1, 0)
                    h_row(b + 1, 1)
                    a_evac(b)
                    h_stats(b + 1, 0)
                    h_stats(b + 1, 1)
                    q_split(b, 0)
                    if is_first(b):
                        split_lo_out(2)
                    h_aggr(b + 1, 0, 2)
                    h_row(b + 1, 2)
                    q_split(b, 1)
                    if is_first(b):
                        split_lo_out(3)
                    h_shift(b + 1, 0, 2)
                    h_row(b + 1, 3)
                    h_stats(b + 1, 2)
                    q_split(b, 2)
                    h_stats(b + 1, 3)
                    h_aggr(b + 1, 2, 2)
                    q_split(b, 3)
                    h_shift(b + 1, 2, 2)
                for c in range(NC - 1):
                    t_split(b + 1, c)
                if last:
                    o_evac(b, 0)
                t_split(b + 1, NC - 1)
                for t in (1, 2, 3) if last else (2, 3, 0, 1):
                    o_evac(b, t)

            for s, n in ((kacc, FREE_ACC), (o_y, FREE_O), (d_y, FREE_DY)):
                dve.sem_inc(s, n)
            v.memset(half[:, 0:1], 1.0).then_inc(cst, 1)
            v.memset(half[:, 1:2], 0.5).then_inc(cst, 1)
            v.memset(ones[:], 1.0).then_inc(cst, 1)
            v.memset(expo[:], -0.5).then_inc(cst, 1)
            dve.wait_ge(c_exp, 1)
            v.tensor_scalar(sc_t[:, 1, :], sc_t[:, 0, :], 1.0, None, ALU.add).then_inc(c_steps, 1)
            dve.wait_ge(c_steps, 1)
            v.reciprocal(sc_t[:, 2, :], sc_t[:, 1, :]).then_inc(c_steps, 1)
            dve.wait_ge(c_steps, 2)
            v.tensor_tensor(sc[:], sc_t[:, 2, :], col[:, COL_C:COL_C + NC * B], ALU.mult).then_inc(c_steps, 1)
            dve.wait_ge(wg_hi_s, 1)
            v.tensor_tensor(wg_r[:, :, NE:2 * NE], col[:, COL_WG:COLS].rearrange("p (k e) -> p k e", k=NC),
                            wg_r[:, :, 0:NE].bitcast(f32), ALU.subtract).then_inc(c_steps, 1)
            x_stats(0, 0, NT)
            x_aggr(0)
            dve.wait_ge(mod_ps, 1)
            v.tensor_scalar(rows[:, 0, :], ps[0:B, 0, :], 1.0, None, ALU.add).then_inc(mod_sb, 1)
            x_shift(0)
            dve.wait_ge(mod_ps, 2)
            v.tensor_copy(rows[:, 1, :], ps[0:B, 1, :]).then_inc(mod_sb, 1)

            def scale_row0(t):
                dve.wait_ge(bc_ps, 1)
                dve.wait_ge(xn_s, t + 1)
                v.tensor_tensor(h1[:, t * D:(t + 1) * D], z[:, t, :], ps[:, 2, :], ALU.mult).then_inc(scaled0_s, 1)

            scale_row0(0)
            scale_row0(1)
            dve.wait_ge(bc_ps, 2)
            h_row(0, 0)
            h_row(0, 1)
            h_stats(0, 0)
            h_stats(0, 1)
            h_aggr(0, 0, 2)
            scale_row0(2)
            scale_row0(3)
            h_shift(0, 0, 2)
            h_row(0, 2)
            h_row(0, 3)
            h_stats(0, 2)
            h_stats(0, 3)
            h_aggr(0, 2, 2)
            dve.wait_ge(mod_ps, 4)
            v.tensor_scalar(cb_col[:].rearrange("p (b c) -> p c b", c=NC),
                            ps[:, 0, 0:NC * B].rearrange("p (c b) -> p c b", c=NC), 1.0, None, ALU.add).then_inc(mod_sb, 1)
            h_shift(0, 2, 2)

            def split_v(k):
                raw, hi = w_raw[1][:, k * D:(k + 1) * D], w_hi[:, WV, k, :]
                dve.wait_ge(wkv_in[k][1], 16)
                v.tensor_copy(hi, raw).then_inc(whi_v, 1)
                dve.wait_ge(whi_v, k + 1)
                v.tensor_tensor(w_lo[:, WV, k, :], raw, hi.bitcast(f32), ALU.subtract).then_inc(wlo_v, 1)

            split_v(0)
            dve.wait_ge(gate_abs_s, 1)
            v.tensor_scalar(sign, ps[0:B, 4:6, :], 0.0, 0.5, ALU.is_ge, ALU.subtract).then_inc(mod_sb, 1)
            dve.wait_ge(mod_sb, 4)
            v.scalar_tensor_tensor(gate_rows, gate_abs, 2 * MIN_GATE, sign, ALU.max, ALU.mult).then_inc(mod_sb, 1)
            t_split(0, 0)
            split_v(1)
            dve.wait_ge(mod_ps, 6)
            v.tensor_copy(sb_col[:].rearrange("p (b c) -> p c b", c=NC),
                          ps[:, 1, 0:NC * B].rearrange("p (c b) -> p c b", c=NC)).then_inc(mod_sb, 1)
            t_split(0, 1)
            for c in range(2, NC):
                split_v(c)
                t_split(0, c)
            split_lo(2)
            dve.wait_ge(const_in, N_CONST)
            dve.wait_ge(row_out, 32)
            attention(0, False)
            dve.wait_ge(ga_in, B * 16)
            with dve.Fori(1, B - 1) as b:
                attention(b, False)
            attention(B - 1, True)
            for t in range(2):
                x2_out(B - 1, t)

            def routing(b):
                dve.wait_ge(lg_ps2, b + 1)
                v.tensor_copy(lg2[:], ps[:, SMALL_BANK, 0:NT * 2 * NE].rearrange("p (t e) -> p t e", t=NT)).then_inc(lg_s, 1)
                dve.wait_ge(lg_s, b * 2 + 1)
                v.tensor_tensor(lg[:], lg2[:, :, 0:NE], lg2[:, :, NE:2 * NE], ALU.add).then_inc(lg_s, 1)
                wait_apart(dve, lg_s, b * 2 + 2)
                for t in range(NT):
                    v.max(top8[:, t, :], lg[:, t, :]).then_inc(top_s, 1)
                dve.wait_ge(top_s, b * 5 + 4)
                v.tensor_tensor(tdif[:], top8[:, :, 0:2], top8[:, :, 0:1].to_broadcast([P, NT, 2]),
                                ALU.subtract).then_inc(top_s, 1)

            def routing_sum(b):
                dve.wait_ge(ex_s, b + 1)
                v.tensor_tensor(tsum[:], tex[:, :, 0], tex[:, :, 1], ALU.add).then_inc(lg_sum, 1)
                dve.wait_ge(lg_sum, b * 3 + 1)
                v.reciprocal(trec[:], tsum[:]).then_inc(lg_sum, 1)
                dve.wait_ge(lg_sum, b * 3 + 2)
                v.tensor_tensor(trw[:], tex[:], trec[:].rearrange("p (t o) -> p t o", o=1).to_broadcast([P, NT, 2]),
                                ALU.mult).then_inc(lg_sum, 1)
                dve.wait_ge(lg_sum, b * 3 + 3)
                v.tensor_tensor(rsum[:], trw[:, :, 0], trw[:, :, 1], ALU.add).then_inc(rsum_s, 1)

            def u_split(b, c):
                dve.wait_ge(u_his, b * NC + c + 1)
                v.scalar_tensor_tensor(g_lo[:, c, :], ps[:, U_BANKS[c % 2], :], 0.0, g_hi[:, c, :].bitcast(f32),
                                       ALU.max, ALU.subtract).then_inc(u_los, 1)

            def add_experts(t):
                n = (B - 1) * NT + t
                e, x = es[:, t % 2, :], xs[:, tok(B - 1, t)]
                dve.wait_ge(es_s, n + 1)
                v.tensor_tensor(e, e, gate_bc[:, (B - 1) * D:], ALU.mult).then_inc(eg_s, 1)
                dve.wait_ge(eg_s, 2 * t + 1)
                v.tensor_tensor(x, x, e, ALU.add).then_inc(eg_s, 1)

            def d_evac_last(i):
                t, part, bank = LAST_PARTS[i]
                y, x = tmp[:, t, part], xs[:, tok(B - 1, t)][:, part]
                dve.wait_ge(d_ps, (B - 1) * NT + i + 1)
                v.tensor_tensor(y, ps[:, bank, part], gate_bc[:, (B - 1) * D:][:, part], ALU.mult).then_inc(d_y, 1)
                dve.wait_ge(d_y, (B - 1) * NT * 2 + i + 1 + FREE_DY)
                v.tensor_tensor(x, x, y, ALU.add).then_inc(last_out, 1)

            def d_evac(b, t):
                n = b * NT + t
                y = tmp[:, t, :]
                dve.wait_ge(d_ps, n + 1)
                dve.wait_ge(es_s, n + 1)
                v.tensor_tensor(y, ps[:, D_BANKS[t % 2], :], es[:, t % 2, :], ALU.add).then_inc(d_y, 1)
                dve.wait_ge(d_y, n * 2 + 1 + FREE_DY)
                v.tensor_tensor(y, y, gate_bc[:, bass.ds(b * D, D)], ALU.mult).then_inc(d_y, 1)
                dve.wait_ge(d_y, n * 2 + 2 + FREE_DY)
                v.tensor_tensor(xs[:, tok(b, t)], xs[:, tok(b, t)], y, ALU.add).then_inc(out_s, 1)

            def ffn(b, last):
                for c in range(NC):
                    u_split(b, c)
                    if c == 0:
                        routing(b)
                    if not last:
                        x2_rows(b + B + 1, c)
                    if c == 1:
                        routing_sum(b)
                if not last:
                    h_aggr(b + B + 1, 0, NT)
                    h_shift(b + B + 1, 0, NT)
                dve.wait_ge(gb_in, B * 16)
                for c in range(NC):
                    if not last:
                        t_split(b + B + 1, c)
                        if c % 2:
                            d_evac(b, c // 2)
                    else:
                        add_experts(c)
                if not last:
                    d_evac(b, 2)
                    d_evac(b, 3)
                else:
                    for i in range(len(LAST_PARTS)):
                        d_evac_last(i)

            with dve.Fori(0, B - 1) as b:
                ffn(b, False)
            ffn(B - 1, True)

        @block.tensor
        def _(pe):
            mm = nc.tensor.matmul

            def three(dst, l_hi, l_lo, r_hi, r_lo, start, stop):
                mm(dst, l_hi, r_hi, start=start, stop=False)
                mm(dst, l_hi, r_lo, start=False, stop=False)
                return mm(dst, l_lo, r_hi, start=False, stop=stop)

            def mod_row(bank, src, sems):
                for k in range(NC):
                    pe.wait_ge(sems[k % len(sems)], 16)
                    last = mm(ps[0:B, bank, :], sc[:, k * B:(k + 1) * B], src[:, k * D:(k + 1) * D],
                              start=(k == 0), stop=(k == NC - 1))
                last.then_inc(mod_ps, 1)

            def mod_col(bank, src, s):
                pe.wait_ge(s, 16)
                for c in range(NC):
                    for k in range(NC):
                        last = mm(ps[:, bank, c * B:(c + 1) * B], src[:, k * D + c * P:k * D + (c + 1) * P],
                                  sc[:, k * B:(k + 1) * B], start=(k == 0), stop=(k == NC - 1))
                last.then_inc(mod_ps, 1)

            def transposes(g, c):
                if c == 0:
                    pe.wait_ge(z_s, g * NT + NT)
                wait(pe, t_full, g * NC + c - 1)
                for t in range(NT):
                    last = nc.tensor.transpose(ps[:, T_BANKS[c % 2], t * P:(t + 1) * P], z[:, t, c * P:(c + 1) * P], idn[:])
                last.then_inc(t_ps, 1)

            def kv_tile(b, t):
                if t == 1:
                    pe.wait_ge(o_y, (b - 1) * NT + 2 + FREE_O)
                if t >= 2:
                    pe.wait_ge(kv_sb, b * NT + t - 1)
                banks = KV_BANKS[t % 2]
                for k in range(NC):
                    if t == 0:
                        pe.wait_ge(t_los, b * NC + k + 1)
                    lo, hi = t_lo[:, k, t * P:(t + 1) * P], t_hi[:, k, t * P:(t + 1) * P]
                    for bank, r, split in zip(banks, (WK, WV), (wlo_k, wlo_v)):
                        if t == 0:
                            pe.wait_ge(split, k + 1)
                        last = three(ps[:, bank, :], hi, lo, w_hi[:, r, k, :], w_lo[:, r, k, :], k == 0, k == NC - 1)
                last.then_inc(kv_ps, 1)

            def feature_chunk(bank, r, c, s, before_last=None):
                for k in range(NC):
                    if before_last and k == NC - 1:
                        before_last()
                    last = three(ps[:, bank, :], w_hi[:, r, k, c * P:(c + 1) * P], w_lo[:, r, k, c * P:(c + 1) * P],
                                 t_hi[:, k, :], t_lo[:, k, :], k == 0, k == NC - 1)
                last.then_inc(s, 1)

            def a_sums(b):
                pe.wait_ge(afold, b * 3 + 3)
                a = ps[:, SMALL_BANK, :]
                mm(a[:, 0:1], pair[:, 0, :], half[:, 1:2], start=True, stop=True)
                mm(a[:, 1:2], pair[:, 1, :], half[:, 1:2], start=True, stop=True)
                mm(a[:, 2:3], acc[:, 2 * P:3 * P], half[:, 0:1], start=True, stop=True)
                mm(a[:, 3:4], acc[:, 3 * P:4 * P], half[:, 0:1], start=True, stop=True).then_inc(a_ps, 1)

            def attention(b, last):
                for t in range(NT):
                    kv_tile(b, t)
                for c in range(NC):
                    if c == 2:
                        pe.wait_ge(kv_sb, b * NT + 3)
                    if c == 0:
                        pe.wait_ge(wlo, 1)
                        pe.wait_ge(t_los, b * NC + NC)
                        pe.wait_ge(o_y, b * NT + FREE_O)
                    feature_chunk(Q_BANKS[c], WQ, c, q_ps, (lambda: a_sums(b)) if c == 2 else None)
                for c in range(NC):
                    pe.wait_ge(q_los, b * NC + c + 1)
                    pe.wait_ge(wlo_out, c + 1)
                    for t in (2, 3, 0, 1) if c == 0 else range(NT):
                        if c == 0 and t == 2:
                            pe.wait_ge(kv_sb, b * NT + NT)
                        if c == 0 and t == 1:
                            pe.wait_ge(q_los, b * NC + 2)
                        done = three(ps[:, O_BANKS[t], :], g_hi[:, c, t * P:(t + 1) * P], g_lo[:, c, t * P:(t + 1) * P],
                                     w_hi[:, WO, c, :], w_lo[:, WO, c, :], c == 0, c == NC - 1)
                        if c == NC - 1:
                            done.then_inc(o_ps, 1)
                    if last:
                        if c in (1, 2):
                            transposes(b + 1, 2 * c - 2)
                            transposes(b + 1, 2 * c - 1)
                    elif c == 2:
                        transposes(b + 1, 0)
                        transposes(b + 1, 1)
                    elif c == 3:
                        transposes(b + 1, 2)
                        transposes(b + 1, 3)

            pe.wait_ge(c_steps, 3)
            mod_row(0, x_slot(2), ca_w)
            mod_row(1, x_slot(3), sa_w)
            for i in range(2):
                pe.wait_ge(mod_sb, i + 1)
                mm(ps[:, 2 + i, :], ones[:], rows[0:1, i, :], start=True, stop=True).then_inc(bc_ps, 1)
            mod_row(4, x_slot(1), wm_in[2:3])
            mod_col(0, gate_bc[:], wm_in[4])
            mod_row(5, x_slot(2), wm_in[5:6])
            pe.wait_ge(ident_in, 16)
            transposes(0, 0)
            transposes(0, 1)
            mod_col(1, x_slot(3), wm_in[3])
            transposes(0, 2)
            transposes(0, 3)
            pe.wait_ge(mod_sb, 6)
            with pe.Fori(0, B - 1) as b:
                attention(b, False)
            attention(B - 1, True)

            def ffn(b, last):
                pe.wait_ge(t_full, (b + B) * NC + NC)
                for k in range(NC):
                    pe.wait_ge(t_los, (b + B) * NC + k + 1)
                    mm(ps[0:2 * NE, SMALL_BANK, :], wg_r[:, k, :], t_hi[:, k, :], start=(k == 0), stop=False)
                    done = mm(ps[0:NE, SMALL_BANK, :], wg_r[:, k, 0:NE], t_lo[:, k, :], start=False, stop=(k == NC - 1))
                done.then_inc(lg_ps, 1)
                pe.wait_ge(wlo, 2)
                for c in range(NC):
                    if c < 2:
                        pe.wait_ge(o_y, (B - 1) * NT + c + 1 + FREE_O)
                        pe.wait_ge(d_y, (b * NT + c - 2) * 2 + 1 + FREE_DY)
                    else:
                        pe.wait_ge(u_los, b * NC + c - 1)
                    feature_chunk(U_BANKS[c % 2], WUP, c, u_ps)
                    if c == 0:
                        wait_apart(pe, lg_t, b + 1)
                        for t in range(NT):
                            done = nc.tensor.transpose(ps[:, SMALL_BANK, t * 2 * NE:(t + 1) * 2 * NE],
                                                       lgt[:, t * P:(t + 1) * P], idn[0:2 * NE, 0:2 * NE])
                        done.then_inc(lg_ps2, 1)
                pe.wait_ge(wlo_expert, NC)
                pe.wait_ge(o_y, B * NT + FREE_O)
                for t in range(NT):
                    for k in range(NC):
                        done = three(ps[:, E_BANKS[t], :], t_hi[:, k, t * P:(t + 1) * P], t_lo[:, k, t * P:(t + 1) * P],
                                     w_hi[:, WEXP, k, :], w_lo[:, WEXP, k, :], k == 0, k == NC - 1)
                    done.then_inc(e_ps, 1)
                if not last:
                    pe.wait_ge(lg_s, b * 2 + 1)
                    transposes(b + B + 1, 0)
                    transposes(b + B + 1, 1)
                whole = [(t, ALL, D_BANKS[t % 2]) for t in range(NT)]
                for i, (t, part, bank) in enumerate(LAST_PARTS if last else whole):
                    if i < 2:
                        pe.wait_ge(u_los, b * NC + NC)
                        pe.wait_ge(wlo_down, NC)
                    elif not last:
                        pe.wait_ge(d_y, (b * NT + t - 2) * 2 + 1 + FREE_DY)
                    elif i == 4:
                        pe.wait_ge(d_y, b * NT * 2 + 1 + FREE_DY)
                    for k in range(NC):
                        done = three(ps[:, bank, part], g_hi[:, k, t * P:(t + 1) * P], g_lo[:, k, t * P:(t + 1) * P],
                                     w_hi[:, WDOWN, k, part], w_lo[:, WDOWN, k, part], k == 0, k == NC - 1)
                    done.then_inc(d_ps, 1)
                    if t == 0 and not last:
                        transposes(b + B + 1, 2)
                        transposes(b + B + 1, 3)

            with pe.Fori(0, B - 1) as b:
                ffn(b, False)
            ffn(B - 1, True)


def layout(inputs):
    import numpy as np
    a = {k: np.asarray(v) for k, v in inputs.items()}
    half_rot = D // 4
    perm = np.concatenate([np.arange(0, 2 * half_rot, 2), np.arange(1, 2 * half_rot, 2), np.arange(2 * half_rot, D)])

    def chunks(m):
        return np.ascontiguousarray(m.reshape(NC, P, -1).transpose(1, 0, 2).reshape(P, -1))

    w_in = a["L0_attn_W_in"].reshape(D, 3, D)[:, :, perm]
    b_in = a["L0_attn_b_in"].reshape(3, D)[:, perm]
    w = [w_in[:, 1], w_in[:, 2], w_in[:, 0], a["L0_attn_W_out"][perm, :],
         a["L0_ffn_W_up"].T, a["L0_ffn_W_expert"], a["L0_ffn_W_down"].T]
    wmod = a["L0_wmod"].reshape(D, NCOMP, D)
    cols = [chunks(v.reshape(D, 1)) for v in (a["L0_attn_gamma"], a["L0_attn_beta"], b_in[0])]
    cols += [chunks(a["L0_c"].T), chunks(a["L0_ffn_W_gate"].T)]
    rot_dim = D // 2
    inv = (1.0 / 10000.0 ** (np.arange(0, rot_dim, 2, dtype=np.float32) / np.float32(rot_dim))).astype(np.float32)
    ang = (np.arange(S, dtype=np.float32)[:, None] * inv[None, :]).astype(np.float64)
    rot = np.concatenate([np.cos(2 * ang), -np.sin(2 * ang)], axis=1).astype(np.float32)
    return {
        "X": np.ascontiguousarray(a["L0_attn_X"]),
        "cols": np.ascontiguousarray(np.concatenate(cols, axis=1)),
        "ident": np.eye(P, dtype=np.float32),
        "rot": np.ascontiguousarray(rot.reshape(NT, P, -1).transpose(1, 0, 2)),
        "w": np.stack([chunks(m) for m in w]),
        "wmod": np.stack([chunks(wmod[:, i]) for i in range(NCOMP)]),
        "brow": np.ascontiguousarray(np.concatenate([b_in[1], b_in[2], a["L0_attn_b_out"]])[None, :]),
    }


def kernel(**inputs):
    import numpy as np
    import concourse.bacc as bacc
    from concourse.bass_utils import run_bass_kernel_spmd

    arrays = layout(inputs)
    nc = bacc.Bacc("TRN2", target_bir_lowering=False, num_devices=1, dynamic_dma_scratch_size=1024)
    args = {k: nc.dram_tensor(f"in_{k}", v.shape, mybir.dt.from_np(v.dtype), kind="ExternalInput").ap()
            for k, v in arrays.items()}
    out = nc.dram_tensor("out_0", (B, S, D), mybir.dt.float32, kind="ExternalOutput").ap()
    build(nc, **args, out=out)
    r = run_bass_kernel_spmd(nc, [{f"in_{k}": v for k, v in arrays.items()}], core_ids=[0])
    return r.results[0]["out_0"]
```
